# Optimizing a Trainium2 kernel written in Bass

```python
import numpy as np
import jax
import jax.numpy as jnp

def _softmax(x, axis=-1):
    return jax.nn.softmax(x, axis=axis)

def _gelu(x):
    return jax.nn.gelu(x, approximate=True)

def _silu(x):
    return jax.nn.silu(x)

def _sigmoid(x):
    return jax.nn.sigmoid(x)

def _layernorm(x, axis=-1, eps=1e-05):
    m = jnp.mean(x, axis=axis, keepdims=True)
    v = jnp.var(x, axis=axis, keepdims=True)
    return (x - m) / jnp.sqrt(v + eps)

def _scatter_add(tgt, idx, src, axis=0):
    return tgt.at[idx].add(src)

def _segment_sum(src, seg, n):
    return jax.ops.segment_sum(src, seg, n)
kernel_name = 'mk_adj_preln_d4_adj_r2_9d65cf'

def setup_inputs(seed: int=0):
    np.random.seed(seed)
    _w = jnp.asarray

    def _rec_inputs():
        import jax
        import jax.numpy as jnp
        _gk = jax.random.key(seed)
        x = -0.003407 + 1.001 * jax.random.normal(jax.random.fold_in(_gk, 1), (32, 256, 64), jnp.float32)
        _a = jax.random.bernoulli(jax.random.fold_in(_gk, 2), 0.015625, (32, 256, 256))
        _a = jnp.logical_or(_a, jnp.swapaxes(_a, -1, -2))
        _a = jnp.logical_or(_a, jnp.eye(256, dtype=bool))
        _af = _a.astype(jnp.float32)
        _af = _af * jax.random.uniform(jax.random.fold_in(_gk, 3), (32, 256, 256), jnp.float32, 0.05, 0.999994)
        adj = _af
        _nm = jnp.ones((32, 256), dtype=bool)
        nodemask = _nm
        return (x, adj, nodemask)
    x, adj, nodemask = _rec_inputs()

    def _L0_gnn_setup():
        import jax, jax.numpy as jnp
        import numpy as np
        B, N, H = (4, 256, 64)
        key = jax.random.key(seed)
        ks = jax.random.split(key, 11)
        s = 0.05
        return {'t': jnp.float32(0.5), 'h': jax.random.normal(ks[0], (B, N, H), dtype=jnp.float32), 'adjacency': jax.random.uniform(ks[1], (B, N, N), dtype=jnp.float32), 'W1': jax.random.normal(ks[2], (2 * H, H), dtype=jnp.float32) * s, 'b1': jax.random.normal(ks[3], (H,), dtype=jnp.float32) * s, 'W2': jax.random.normal(ks[4], (H, H), dtype=jnp.float32) * s, 'b2': jax.random.normal(ks[5], (H,), dtype=jnp.float32) * s, 'E1': jax.random.normal(ks[6], (2 * H, H), dtype=jnp.float32) * s, 'be1': jax.random.normal(ks[7], (H,), dtype=jnp.float32) * s, 'E2': jax.random.normal(ks[8], (H, 1), dtype=jnp.float32) * s, 'be2': jax.random.normal(ks[9], (1,), dtype=jnp.float32) * s}
    _L0_gnn_all = _L0_gnn_setup()
    _L0_gnn_in = {k: v for k, v in _L0_gnn_all.items() if k in ('t', 'W1', 'b1', 'W2', 'b2', 'E1', 'be1', 'E2', 'be2')}
    del _L0_gnn_all

    def _L1_gnn_setup():
        import jax, jax.numpy as jnp
        import numpy as np
        TAUS = [0.25, 0.5, 0.75]
        QWEIGHTS = [0.25, 0.5, 0.25]
        T_THRESH = 10
        K_DIL = 2
        EPS_GIN = 0.0

        def _dilate_adj(adj, mask):
            B, N, _ = adj.shape
            eye = jnp.eye(N, dtype=bool)
            adj_ = jnp.where(eye[None], 1.0, adj)
            nb = (adj_ > 0) & (~eye)[None]
            m = nb.sum(-1)
            rank = jnp.cumsum(nb, axis=-1) - 1
            skip = jnp.where(m > T_THRESH, (m + K_DIL - 1) // K_DIL, 1)
            do_dil = (skip > 1) & mask
            removed = nb & do_dil[..., None] & ((rank + 1) % skip[..., None] == 0)
            rem = removed | jnp.swapaxes(removed, 1, 2)
            return jnp.where(rem, 0.0, adj_)

        def _weighted_nanquantile_agg(x, valid):
            B, N, C = x.shape
            big = jnp.finfo(x.dtype).max / 4
            vals = jnp.where(valid[..., None], x[:, None, :, :], big)
            sv = jnp.sort(vals, axis=2)
            m = valid.sum(-1)
            mf = m.astype(x.dtype)

            def gather(idx):
                idxb = jnp.broadcast_to(idx[:, :, None, None], (B, N, 1, C))
                return jnp.take_along_axis(sv, idxb, axis=2)[:, :, 0, :]
            agg = jnp.zeros_like(x)
            for tau, wt in zip(TAUS, QWEIGHTS):
                pos = jnp.clip(tau * (mf - 1.0), 0.0)
                lo = jnp.floor(pos).astype(jnp.int32)
                hi = jnp.ceil(pos).astype(jnp.int32)
                frac = (pos - lo.astype(x.dtype))[..., None]
                q = gather(lo) * (1.0 - frac) + gather(hi) * frac
                agg = agg + wt * q
            return jnp.where((m > 0)[..., None], agg, 0.0)
        key = jax.random.key(seed)
        k0, k1, k2, k3 = jax.random.split(key, 4)
        B, N, C, H, CO = (4, 256, 64, 128, 64)
        x = jax.random.normal(k0, (B, N, C), dtype=jnp.float32)
        u = jax.random.uniform(k1, (B, N, N))
        a = (u < 0.03).astype(jnp.float32)
        adj = jnp.maximum(a, jnp.swapaxes(a, 1, 2))
        mask = jnp.broadcast_to(jnp.arange(N) < N - 32, (B, N))
        W1 = jax.random.normal(k2, (C, H), dtype=jnp.float32) * (1.0 / np.sqrt(C))
        b1 = jnp.zeros((H,), dtype=jnp.float32)
        W2 = jax.random.normal(k3, (H, CO), dtype=jnp.float32) * (1.0 / np.sqrt(H))
        b2 = jnp.zeros((CO,), dtype=jnp.float32)
        return {'x': x, 'adj': adj, 'mask': mask, 'W1': W1, 'b1': b1, 'W2': W2, 'b2': b2}
    _L1_gnn_all = _L1_gnn_setup()
    _L1_gnn_in = {k: v for k, v in _L1_gnn_all.items() if k in ('W1', 'b1', 'W2', 'b2')}
    del _L1_gnn_all

    def _L2_gnn_setup():
        import jax, jax.numpy as jnp
        import numpy as np
        key = jax.random.key(seed)
        ks = jax.random.split(key, 6)
        B, N, F, H, O = (2, 256, 64, 192, 64)
        x = jax.random.normal(ks[0], (B, N, F), dtype=jnp.float32)
        adj = jax.random.normal(ks[1], (B, N, N), dtype=jnp.float32)
        W1 = jax.random.normal(ks[2], (2 * F, H), dtype=jnp.float32) * (1.0 / np.sqrt(2 * F))
        b1 = jax.random.normal(ks[3], (H,), dtype=jnp.float32) * 0.02
        W2 = jax.random.normal(ks[4], (H, O), dtype=jnp.float32) * (1.0 / np.sqrt(H))
        b2 = jax.random.normal(ks[5], (O,), dtype=jnp.float32) * 0.02
        return {'x': x, 'adj': adj, 'W1': W1, 'b1': b1, 'W2': W2, 'b2': b2}
    _L2_gnn_all = _L2_gnn_setup()
    _L2_gnn_in = {k: v for k, v in _L2_gnn_all.items() if k in ('W1', 'b1', 'W2', 'b2')}
    del _L2_gnn_all

    def _L3_gnn_setup():
        import jax, jax.numpy as jnp
        import numpy as np
        MIN_NORM = 1e-15
        BALL_EPS = 0.004
        C = 1.0
        CLAMP = 1000000.0

        def _artanh(x):
            return jnp.arctanh(jnp.clip(x, -1.0 + 1e-07, 1.0 - 1e-07))

        def _norm(x):
            return jnp.maximum(jnp.linalg.norm(x, axis=-1, keepdims=True), MIN_NORM)

        def mobius_add(x, y, c):
            x2 = jnp.sum(x * x, axis=-1, keepdims=True)
            y2 = jnp.sum(y * y, axis=-1, keepdims=True)
            xy = jnp.sum(x * y, axis=-1, keepdims=True)
            num = (1.0 + 2.0 * c * xy + c * y2) * x + (1.0 - c * x2) * y
            den = 1.0 + 2.0 * c * xy + c * c * x2 * y2
            return num / jnp.maximum(den, MIN_NORM)

        def lambda_x(x, c):
            return 2.0 / jnp.maximum(1.0 - c * jnp.sum(x * x, axis=-1, keepdims=True), MIN_NORM)

        def logmap(p1, p2, c):
            sub = mobius_add(-p1, p2, c)
            sub_norm = _norm(sub)
            sqrt_c = c ** 0.5
            return 2.0 / sqrt_c / lambda_x(p1, c) * _artanh(sqrt_c * sub_norm) * sub / sub_norm

        def expmap(u, p, c):
            sqrt_c = c ** 0.5
            u_norm = _norm(u)
            second = jnp.tanh(sqrt_c / 2.0 * lambda_x(p, c) * u_norm) * u / (sqrt_c * u_norm)
            return mobius_add(p, second, c)

        def proj(x, c):
            norm = _norm(x)
            maxnorm = (1.0 - BALL_EPS) / c ** 0.5
            return jnp.where(norm > maxnorm, x / norm * maxnorm, x)
        key = jax.random.key(seed)
        kx, ka, kw = jax.random.split(key, 3)
        B, N, D = (2, 384, 64)
        x = proj(0.2 * jax.random.normal(kx, (B, N, D), dtype=jnp.float32), C)
        adj = (jax.random.uniform(ka, (B, N, N), dtype=jnp.float32) < 0.05).astype(jnp.float32)
        att_W = jax.random.normal(kw, (2 * D, 1), dtype=jnp.float32) * (1.0 / np.sqrt(2 * D))
        att_b = jnp.zeros((1,), dtype=jnp.float32)
        return {'x': x, 'adj': adj, 'att_W': att_W, 'att_b': att_b}
    _L3_gnn_all = _L3_gnn_setup()
    _L3_gnn_in = {k: v for k, v in _L3_gnn_all.items() if k in ('att_W', 'att_b')}
    del _L3_gnn_all
    return {'x': x, 'adj': adj, 'nodemask': nodemask, 'L0_gnn_t': _L0_gnn_in['t'], 'L0_gnn_W1': _L0_gnn_in['W1'], 'L0_gnn_b1': _L0_gnn_in['b1'], 'L0_gnn_W2': _L0_gnn_in['W2'], 'L0_gnn_b2': _L0_gnn_in['b2'], 'L0_gnn_E1': _L0_gnn_in['E1'], 'L0_gnn_be1': _L0_gnn_in['be1'], 'L0_gnn_E2': _L0_gnn_in['E2'], 'L0_gnn_be2': _L0_gnn_in['be2'], 'L1_gnn_W1': _L1_gnn_in['W1'], 'L1_gnn_b1': _L1_gnn_in['b1'], 'L1_gnn_W2': _L1_gnn_in['W2'], 'L1_gnn_b2': _L1_gnn_in['b2'], 'L2_gnn_W1': _L2_gnn_in['W1'], 'L2_gnn_b1': _L2_gnn_in['b1'], 'L2_gnn_W2': _L2_gnn_in['W2'], 'L2_gnn_b2': _L2_gnn_in['b2'], 'L3_gnn_att_W': _L3_gnn_in['att_W'], 'L3_gnn_att_b': _L3_gnn_in['att_b']}

def reference(x, adj, nodemask, L0_gnn_t, L0_gnn_W1, L0_gnn_b1, L0_gnn_W2, L0_gnn_b2, L0_gnn_E1, L0_gnn_be1, L0_gnn_E2, L0_gnn_be2, L1_gnn_W1, L1_gnn_b1, L1_gnn_W2, L1_gnn_b2, L2_gnn_W1, L2_gnn_b1, L2_gnn_W2, L2_gnn_b2, L3_gnn_att_W, L3_gnn_att_b):
    import jax
    import jax.numpy as jnp

    def _L0_gnn_ref(t, h, adjacency, W1, b1, W2, b2, E1, be1, E2, be2):
        import jax, jax.numpy as jnp
        import numpy as np
        B, N, H = (4, 256, 64)
        messages = jnp.einsum('bij,bjh->bih', adjacency, h)
        node_in = jnp.concatenate([h, messages], axis=-1)
        dh = jnp.tanh(node_in @ W1 + b1) @ W2 + b2
        hd = h.shape[-1]
        pi = h @ E1[:hd]
        pj = h @ E1[hd:]
        eh = jnp.tanh(pi[:, :, None, :] + pj[:, None, :, :] + be1)
        edge_updates = (eh @ E2)[..., 0] + be2[0]
        _ = adjacency + edge_updates
        return dh

    def _L1_gnn_ref(x, adj, mask, W1, b1, W2, b2):
        import jax, jax.numpy as jnp
        import numpy as np
        TAUS = [0.25, 0.5, 0.75]
        QWEIGHTS = [0.25, 0.5, 0.25]
        T_THRESH = 10
        K_DIL = 2
        EPS_GIN = 0.0

        def _dilate_adj(adj, mask):
            B, N, _ = adj.shape
            eye = jnp.eye(N, dtype=bool)
            adj_ = jnp.where(eye[None], 1.0, adj)
            nb = (adj_ > 0) & (~eye)[None]
            m = nb.sum(-1)
            rank = jnp.cumsum(nb, axis=-1) - 1
            skip = jnp.where(m > T_THRESH, (m + K_DIL - 1) // K_DIL, 1)
            do_dil = (skip > 1) & mask
            removed = nb & do_dil[..., None] & ((rank + 1) % skip[..., None] == 0)
            rem = removed | jnp.swapaxes(removed, 1, 2)
            return jnp.where(rem, 0.0, adj_)

        def _weighted_nanquantile_agg(x, valid):
            B, N, C = x.shape
            big = jnp.finfo(x.dtype).max / 4
            vals = jnp.where(valid[..., None], x[:, None, :, :], big)
            sv = jnp.sort(vals, axis=2)
            m = valid.sum(-1)
            mf = m.astype(x.dtype)

            def gather(idx):
                idxb = jnp.broadcast_to(idx[:, :, None, None], (B, N, 1, C))
                return jnp.take_along_axis(sv, idxb, axis=2)[:, :, 0, :]
            agg = jnp.zeros_like(x)
            for tau, wt in zip(TAUS, QWEIGHTS):
                pos = jnp.clip(tau * (mf - 1.0), 0.0)
                lo = jnp.floor(pos).astype(jnp.int32)
                hi = jnp.ceil(pos).astype(jnp.int32)
                frac = (pos - lo.astype(x.dtype))[..., None]
                q = gather(lo) * (1.0 - frac) + gather(hi) * frac
                agg = agg + wt * q
            return jnp.where((m > 0)[..., None], agg, 0.0)
        dtp = x.dtype
        adj_d = _dilate_adj(adj, mask)
        agg = _weighted_nanquantile_agg(x, adj_d > 0)
        out = (1.0 + EPS_GIN) * x + agg
        h = jax.nn.relu(jnp.einsum('bnc,ch->bnh', out, W1) + b1)
        y = jnp.einsum('bnh,ho->bno', h, W2) + b2
        return y * mask[..., None].astype(dtp)

    def _L2_gnn_ref(x, adj, W1, b1, W2, b2):
        import jax, jax.numpy as jnp
        import numpy as np
        F = x.shape[-1]
        mask = (adj > 0.0).astype(x.dtype)
        W1a, W1b = (W1[:F], W1[F:])
        xj_proj = x @ W1a
        diff = x[:, :, None, :] - x[:, None, :, :]
        h = jax.nn.relu(xj_proj[:, :, None, :] + diff @ W1b + b1)
        hm = jnp.einsum('bjkh,bjk->bjh', h, mask)
        deg = jnp.sum(mask, axis=-1)
        return hm @ W2 + deg[..., None] * b2

    def _L3_gnn_ref(x, adj, att_W, att_b):
        import jax, jax.numpy as jnp
        import numpy as np
        MIN_NORM = 1e-15
        BALL_EPS = 0.004
        C = 1.0
        CLAMP = 1000000.0

        def _artanh(x):
            return jnp.arctanh(jnp.clip(x, -1.0 + 1e-07, 1.0 - 1e-07))

        def _norm(x):
            return jnp.maximum(jnp.linalg.norm(x, axis=-1, keepdims=True), MIN_NORM)

        def mobius_add(x, y, c):
            x2 = jnp.sum(x * x, axis=-1, keepdims=True)
            y2 = jnp.sum(y * y, axis=-1, keepdims=True)
            xy = jnp.sum(x * y, axis=-1, keepdims=True)
            num = (1.0 + 2.0 * c * xy + c * y2) * x + (1.0 - c * x2) * y
            den = 1.0 + 2.0 * c * xy + c * c * x2 * y2
            return num / jnp.maximum(den, MIN_NORM)

        def lambda_x(x, c):
            return 2.0 / jnp.maximum(1.0 - c * jnp.sum(x * x, axis=-1, keepdims=True), MIN_NORM)

        def logmap(p1, p2, c):
            sub = mobius_add(-p1, p2, c)
            sub_norm = _norm(sub)
            sqrt_c = c ** 0.5
            return 2.0 / sqrt_c / lambda_x(p1, c) * _artanh(sqrt_c * sub_norm) * sub / sub_norm

        def expmap(u, p, c):
            sqrt_c = c ** 0.5
            u_norm = _norm(u)
            second = jnp.tanh(sqrt_c / 2.0 * lambda_x(p, c) * u_norm) * u / (sqrt_c * u_norm)
            return mobius_add(p, second, c)

        def proj(x, c):
            norm = _norm(x)
            maxnorm = (1.0 - BALL_EPS) / c ** 0.5
            return jnp.where(norm > maxnorm, x / norm * maxnorm, x)
        c = C
        b, n, d = x.shape
        x_i = x[:, :, None, :]
        x_j = x[:, None, :, :]
        x_local = logmap(x_i, x_j, c)
        x_self = logmap(x, x, c)
        feats = jnp.concatenate([jnp.broadcast_to(x_self[:, :, None, :], x_local.shape), x_local], axis=-1)
        logits = jnp.einsum('bijk,ko->bijo', feats, att_W)[..., 0] + att_b[0]
        att = jax.nn.sigmoid(logits) * adj
        support_t = jnp.einsum('bij,bijd->bid', att, x_local)
        support_t = jnp.clip(support_t, -CLAMP, CLAMP)
        return proj(expmap(support_t, x, c), c)
    h = jnp.maximum(_layernorm(x, axis=-1), 0.0)
    x = x + _L0_gnn_ref(L0_gnn_t, h, adj, L0_gnn_W1, L0_gnn_b1, L0_gnn_W2, L0_gnn_b2, L0_gnn_E1, L0_gnn_be1, L0_gnn_E2, L0_gnn_be2)
    h = jnp.maximum(_layernorm(x, axis=-1), 0.0)
    x = x + _L1_gnn_ref(h, adj, nodemask, L1_gnn_W1, L1_gnn_b1, L1_gnn_W2, L1_gnn_b2)
    h = jnp.maximum(_layernorm(x, axis=-1), 0.0)
    x = x + _L2_gnn_ref(h, adj, L2_gnn_W1, L2_gnn_b1, L2_gnn_W2, L2_gnn_b2)
    h = jnp.maximum(_layernorm(x, axis=-1), 0.0)
    x = x + _L3_gnn_ref(h, adj, L3_gnn_att_W, L3_gnn_att_b)
    return x

_drawn_inputs = setup_inputs


def setup_inputs(seed=0):
    import zlib

    import numpy as np

    out = dict(_drawn_inputs(seed))
    spreads = {'L1_gnn_b1': (0.0, 0.1), 'L1_gnn_b2': (0.0, 0.1)}
    factors = {'L0_gnn_b1': 3.383}
    for name, (base, spread) in spreads.items():
        noise = np.random.default_rng([zlib.crc32(name.encode()), seed]).standard_normal(out[name].shape)
        drawn = base * np.exp(spread * noise) if base else spread * noise
        out[name] = jnp.asarray(drawn.astype(out[name].dtype))
    for name, factor in factors.items():
        out[name] = (out[name] * factor).astype(out[name].dtype)
    return out
```

```python
import numpy as np
import concourse.bass as bass
import concourse.mybir as mybir
from concourse.alu_op_type import AluOpType as ALU
from contextlib import ExitStack

F32 = mybir.dt.float32
BF16 = mybir.dt.bfloat16
I32 = mybir.dt.int32
U8 = mybir.dt.uint8
ACT = mybir.ActivationFunctionType
AX = mybir.AxisListType

B, N, F = 32, 256, 64
P = 128
HALVES = N // P
G = 8
NG = B // G
T = G * HALVES
H1, H2 = 128, 192
K1 = 20
K2 = 24
PAIRS = G // 2
LAYERS = 4
TAUS = [(0.25, 0.25), (0.5, 0.5), (0.75, 0.25)]
DILATE_OVER = 10.0
FAR = 1000.0
ROUND = 8388608.0
EPS = 1e-5
MIN_NORM = 1e-15
MIN_SQ = 1e-18
CLIP = float(np.float32(1.0 - 1e-7))
MAXNORM = 1.0 - 0.004
CLAMP = 1e6
FX = F + 3


def sorting_network(n, outputs):
    size = 1
    while size < n:
        size *= 2
    layers, p = [], 1
    while p < size:
        k = p
        while k >= 1:
            layers.append([(i + j, i + j + k) for j in range(k % p, size - k, 2 * k)
                           for i in range(min(k, size - j - k))
                           if (i + j) // (2 * p) == (i + j + k) // (2 * p) and i + j + k < n])
            k //= 2
        p *= 2
    needed = set(range(outputs))
    kept = []
    for layer in reversed(layers):
        out = [(a, b, a in needed, b in needed) for a, b in layer if a in needed or b in needed]
        for a, b, _, _ in out:
            needed |= {a, b}
        kept.append(out)
    return [layer for layer in reversed(kept) if layer]


def program(nc, x, adj, nodemask, W1_0, b1_0, W2_0, b2_0, W1_1, b1_1, W2_1, b2_1, W1_2, b1_2, W2_2, b2_2,
            att_W, att_b, out):
    D_USED = int(np.ceil(0.75 * (K1 - 1))) + 1
    NETWORK = sorting_network(K1, D_USED)
    SPARE = 6
    NBUF = K1 + SPARE
    SORT_OPS = sum(hi + lo for layer in NETWORK for _, _, hi, lo in layer)

    ctx = ExitStack()
    with ctx:
        def sb(name, shape, dt=F32):
            return ctx.enter_context(nc.sbuf_tensor(name, shape, dt))

        def sem(name):
            return ctx.enter_context(nc.semaphore(name))

        identf = sb("identf", [P, P])
        identb = sb("identb", [P, P], BF16)
        tri = sb("tri", [P, P], BF16)
        onesb = sb("onesb", [P, P], BF16)
        onesf = sb("onesf", [P, P])
        eye = sb("eye", [P, HALVES, N], BF16)
        noteye = sb("noteye", [P, HALVES, N], BF16)
        place_i = sb("place_i", [P, K1], I32)
        place = sb("place", [P, K1])
        w1_0 = sb("w1_0", [F, 2, F])
        w2_0 = sb("w2_0", [F, F])
        w1_1 = sb("w1_1", [F, H1])
        w2_1 = sb("w2_1", [H1, F])
        w1_2 = sb("w1_2", [F, 2, H2])
        wsum_2 = sb("wsum_2", [F, H2])
        w2_2 = sb("w2_2", [H2 // 2, 2, F])
        bias0 = sb("bias0", [F, 1])
        bias1 = sb("bias1", [H1, 1])
        brow = sb("brow", [1, 2, F])
        b2_all = sb("b2_all", [P, F])
        brow2 = sb("brow2", [1, H2])
        att_w = sb("att_w", [P, 2, F])
        att_c = sb("att_c", [P, 1])
        mask_in = sb("mask_in", [B * HALVES, P], U8)
        mask_f = sb("mask_f", [B * HALVES, P])
        mask_col = sb("mask_col", [P, NG, T])
        over = sb("over", [P, 2])
        is_long = sb("is_long", [1, 1], I32)

        adj_in = sb("adj_in", [P, T // 2, N])
        adjT = sb("adjT", [P, G, HALVES, N])
        mask_row8 = sb("mask_row8", [P, G * N], U8)
        slot1 = sb("slot1", [P, G, HALVES, N], BF16)
        slot2 = sb("slot2", [P, G, HALVES, N], BF16)
        x_in = sb("x_in", [P, T, F])
        xs = sb("xs", [P, T, F])
        h = sb("h", [P, T, F])
        hp = sb("hp", [P, T, 3, F], BF16)
        SEL = 2
        pick = sb("pick", [P, SEL, G, HALVES, N], BF16)
        feat = sb("feat", [F, 2, 2, N])
        tanh_t = sb("tanh_t", [F, 2, N])
        hid = sb("hid", [P, 2, N])
        degs = sb("degs", [P, 2, T])
        wq = sb("wq", [P, T, K1])
        wt = sb("wt", [P, T, K1])
        stat = sb("stat", [P, 4, T])
        sm = sb("sm", [P, 24, T])
        cT = sb("cT", [T, P])
        scr = sb("scr", [P, NBUF, T * F])

        def region(byte, shape, dt=F32):
            n = int(np.prod(shape[1:]))
            flat = scr[:, :, :].rearrange("p a b -> p (a b)")
            if dt == BF16:
                flat = flat.bitcast(BF16)
                v = flat[0:shape[0], byte // 2:byte // 2 + n]
            else:
                v = flat[0:shape[0], byte // 4:byte // 4 + n]
            names = "abcd"[:len(shape) - 1]
            if len(shape) == 2:
                return v
            return v.rearrange(f"p ({' '.join(names)}) -> p {' '.join(names)}",
                               **{c: s for c, s in zip(names, shape[1:])})

        KB = 1024
        PAIR = [P, G, HALVES, N]
        any_m = region(0, PAIR, BF16)
        nb_m = region(8 * KB, PAIR, BF16)
        val_m = region(16 * KB, PAIR, BF16)
        gone = region(24 * KB, PAIR, BF16)
        at1 = region(32 * KB, PAIR, BF16)
        at2 = region(40 * KB, PAIR, BF16)
        cnt = region(48 * KB, [P, G, N])
        rank1 = region(56 * KB, [P, G, N])
        on = region(64 * KB, [P, G, N])
        rank2 = region(72 * KB, [P, G, N])
        LN_AT = (NBUF - 2) * T * F * 4
        xc = region(LN_AT, [P, T, F])
        sq = region(LN_AT + 4 * KB, [P, T, F])
        AGG = 0
        u2 = region(0, [P, T, H2])
        v2 = region(12 * KB, [P, T, H2])
        vp = region(24 * KB, [P, T, 3, H2], BF16)
        acc2 = region(42 * KB, [P, T, H2])
        t2 = region(54 * KB, [P, 2, 4, H2])
        rest2 = region(60 * KB, [P, T, H2])
        acc2T = region(72 * KB, [H2 // 2, 2, 2 * N])
        bn = region(0, PAIR)
        bd = region(16 * KB, PAIR)
        bq = region(32 * KB, PAIR)
        bb = region(48 * KB, PAIR)
        bz = region(64 * KB, PAIR)
        tok = region(80 * KB, [P, 4, T, FX])
        cb = slot1[:, :, :, :].rearrange("p g a n -> p (g a n)").bitcast(F32).rearrange("p (g n) -> p g n", g=G)
        LR = pick[:, :, :, :, :].rearrange("p s g a n -> p (s g a n)").bitcast(F32)[0:FX, 0:2 * 4 * N].rearrange(
            "p (r m n) -> p r m n", r=2, m=4)
        feat3 = region(0, [P, T, F + 1])
        sp = region(8 * KB, [P, T, F + 1])
        y3 = region(16 * KB, [P, T, F])
        z3 = region(20 * KB, [P, T, F])
        w3 = region(24 * KB, [P, T, F])

        PICKS2 = 4
        pick2 = pick[:, :, :, :, :].rearrange("p s g a n -> p (s g a n)")[:, 0:PICKS2 * 4 * N].rearrange(
            "p (s n) -> p s n", s=PICKS2)

        def f2(t):
            return t.rearrange("p a n -> p (a n)")

        ps = ctx.enter_context(nc.psum_tensor("ps", [P, 8, 512], F32))
        psb = ps[:, :, :].bitcast(BF16)

        LONG = 24 * KB
        all_valid = region(LONG, [P, N])
        all_left = region(LONG + KB, [P, N])
        all_sorted = region(LONG + 2 * KB, [P, N])
        all_place = region(LONG + 3 * KB, [P, N])
        all_w = region(LONG + 4 * KB, [P, N])
        all_wt = region(LONG + 5 * KB, [P, N])
        all_prod = region(LONG + 6 * KB, [P, N])
        all_agg = region(LONG + 8 * KB, [P, T, F])
        acc2_rest = region(LONG + 48 * KB, [P, T, H2])

        const_loaded = sem("const_loaded")
        const_made = sem("const_made")
        const_cast = sem("const_cast")
        mask_T = sem("mask_T")
        adj_loaded = sem("adj_loaded")
        x_loaded = sem("x_loaded")
        mrow_loaded = sem("mrow_loaded")
        out_stored = sem("out_stored")
        x_free = sem("x_free")
        adjT_ps = sem("adjT_ps")
        adjT_sb = sem("adjT_sb")
        nb_ready = sem("nb_ready")
        cnt_ps = sem("cnt_ps")
        cnt_sb = sem("cnt_sb")
        nbcum_ps = sem("nbcum_ps")
        gone_ready = sem("gone_ready")
        goneT_ps = sem("goneT_ps")
        val_ready = sem("val_ready")
        cum1_ps = sem("cum1_ps")
        slot1_ready = sem("slot1_ready")
        cum2_ps = sem("cum2_ps")
        slot2_ready = sem("slot2_ready")
        deg_ps = sem("deg_ps")
        var_ready = sem("var_ready")
        std_ready = sem("std_ready")
        h0_ready = sem("h0_ready")
        feat0_ps = sem("feat0_ps")
        feat0_sb = sem("feat0_sb")
        pre0_ps = sem("pre0_ps")
        tanh_sb = sem("tanh_sb")
        dh0_ps = sem("dh0_ps")
        x1_ready = sem("x1_ready")
        parts1_ready = sem("parts1_ready")
        pick1_ready = sem("pick1_ready")
        fetched1_ps = sem("fetched1_ps")
        fetched1_sb = sem("fetched1_sb")
        sorted_ops = sem("sorted_ops")
        agg_ready = sem("agg_ready")
        aggT_ps = sem("aggT_ps")
        aggT_sb = sem("aggT_sb")
        hid_ps = sem("hid_ps")
        hid_sb = sem("hid_sb")
        y1_ps = sem("y1_ps")
        h2_ready = sem("h2_ready")
        h2T_ps = sem("h2T_ps")
        h2T_sb = sem("h2T_sb")
        uv_ps = sem("uv_ps")
        uv_sb = sem("uv_sb")
        parts2_ready = sem("parts2_ready")
        pick2_ready = sem("pick2_ready")
        fetched2_ps = sem("fetched2_ps")
        taken2 = sem("taken2")
        summed2 = sem("summed2")
        acc2T_ps = sem("acc2T_ps")
        acc2T_sb = sem("acc2T_sb")
        y2_ps = sem("y2_ps")
        tok_ready = sem("tok_ready")
        cT_ps = sem("cT_ps")
        cT_sb = sem("cT_sb")
        cb_ps = sem("cb_ps")
        cb_sb = sem("cb_sb")
        LR_ps = sem("LR_ps")
        LR_sb = sem("LR_sb")
        pair_ps = sem("pair_ps")
        clamped = sem("clamped")
        logs_sb = sem("logs_sb")
        hz_sb = sem("hz_sb")
        qp_ready = sem("qp_ready")
        exps_sb = sem("exps_sb")
        s_clipped = sem("s_clipped")
        log1_sb = sem("log1_sb")
        diff_ready = sem("diff_ready")
        z_ready = sem("z_ready")
        sig_sb = sem("sig_sb")
        att_ready = sem("att_ready")
        weight_ready = sem("weight_ready")
        feat3_ready = sem("feat3_ready")
        support_ps = sem("support_ps")
        support_sb = sem("support_sb")
        small_ready = sem("small_ready")
        small_done = sem("small_done")
        mask_cast = sem("mask_cast")
        over_ready = sem("over_ready")
        over_ps = sem("over_ps")
        long_ready = sem("long_ready")
        valid_ps = sem("valid_ps")
        valid_used = sem("valid_used")
        row_ps = sem("row_ps")
        row_used = sem("row_used")
        more_picked = sem("more_picked")
        more_ps = sem("more_ps")
        more_summed = sem("more_summed")
        out_ready = sem("out_ready")

        SMALL = 5
        X2, WL, WS, BM, LAM, LB, LW, NLW, CC, DD, DF, SN, S0, S1, S2, S3, S4, S5, NORM, DK, M1, MC = range(22)
        block = ctx.enter_context(nc.Block())

        @block.sync
        def _(sync):
            for s in (adjT_ps, x_free, support_sb, att_ready, row_used):
                sync.sem_inc(s, 1)
            sync.sem_inc(out_stored, 16)

            def const(dst, src):
                sync.dma_start(dst, src).then_inc(const_loaded, 16)
            const(w1_0[:, :, :], W1_0.rearrange("(a c) o -> c a o", a=2))
            const(w2_0[:, :], W2_0)
            const(w1_1[:, :], W1_1)
            const(w2_1[:, :], W2_1)
            const(w1_2[:, :, :], W1_2.rearrange("(a c) o -> c a o", a=2))
            const(w2_2[:, :, :], W2_2.rearrange("(a c) o -> c a o", a=2))
            const(bias0[:, :], b1_0.rearrange("(c o) -> c o", o=1))
            const(bias1[:, :], b1_1.rearrange("(c o) -> c o", o=1))
            const(brow[:, 0, :], b2_0.rearrange("(o c) -> o c", o=1))
            const(brow[:, 1, :], b2_1.rearrange("(o c) -> o c", o=1))
            const(b2_all[:, :], b2_2.rearrange("(o c) -> o c", o=1).broadcast_to([P, F]))
            const(brow2[:, :], b1_2.rearrange("(o c) -> o c", o=1))
            const(att_w[:, 0, :], att_W[0:F, :].rearrange("c o -> o c").broadcast_to([P, F]))
            const(att_w[:, 1, :], att_W[F:2 * F, :].rearrange("c o -> o c").broadcast_to([P, F]))
            const(att_c[:, :], att_b.rearrange("(o c) -> o c", o=1).broadcast_to([P, 1]))
            const(mask_in[:, :], nodemask.rearrange("b (t p) -> (b t) p", p=P))
            x_v = x.rearrange("(g b) (t p) c -> p g (b t) c", g=NG, p=P)
            adj_v = adj.rearrange("(g b) (t p) j -> p g (b t) j", g=NG, p=P)
            out_v = out.rearrange("(g b) (t p) c -> p g (b t) c", g=NG, p=P)
            mrow_v = nodemask.rearrange("(g b) n -> g (b n)", g=NG)
            with sync.Fori(0, NG) as g:
                for b in range(G):
                    if b % (G // 2) == 0:
                        sync.wait_ge(adjT_ps, g * G + b + 1)
                    at = 2 * b % (T // 2)
                    sync.dma_start(adj_in[:, at:at + 2, :],
                                   adj_v[:, bass.ds(g, 1), 2 * b:2 * b + 2, :].rearrange("p o t j -> p (o t) j")
                                   ).then_inc(adj_loaded, 16)
                sync.wait_ge(x_free, g + 1)
                sync.dma_start(x_in[:, :, :], x_v[:, bass.ds(g, 1)].rearrange("p o t c -> p (o t) c")
                               ).then_inc(x_loaded, 16)
                sync.dma_start(mask_row8[:, :], mrow_v[bass.ds(g, 1), :].broadcast_to([P, G * N])
                               ).then_inc(mrow_loaded, 16)

        @block.gpsimd
        def _(pool):
            g_ = nc.gpsimd
            made = [0]

            def make(ins):
                made[0] += 1
                ins.then_inc(const_made, 1)

            make(g_.memset(identf[:, :], 0.0))
            make(g_.memset(identb[:, :], 0.0))
            make(g_.memset(tri[:, :], 1.0))
            make(g_.memset(onesb[:, :], 1.0))
            make(g_.memset(onesf[:, :], 1.0))
            make(g_.memset(eye[:, :, :], 0.0))
            make(g_.memset(noteye[:, :, :], 1.0))
            pool.wait_ge(const_made, 7)
            for m in (identf, identb):
                make(g_.affine_select(out=m[:, :], in_=m[:, :], compare_op=ALU.not_equal, fill=1.0, base=0,
                                      pattern=[[-1, P]], channel_multiplier=1))
            make(g_.affine_select(out=tri[:, :], in_=tri[:, :], compare_op=ALU.is_ge, fill=0.0, base=0,
                                  pattern=[[1, P]], channel_multiplier=-1))
            for m, v in ((eye, 1.0), (noteye, 0.0)):
                make(g_.affine_select(out=m[:, :, :], in_=m[:, :, :], compare_op=ALU.not_equal, fill=v, base=0,
                                      pattern=[[P, HALVES], [-1, N]], channel_multiplier=1))
            make(g_.iota(place_i[:, :], pattern=[[1, K1]], base=0, channel_multiplier=0))
            assert made[0] == 13
            with pool.Fori(0, NG) as g:
                for i in range(G + 2):
                    if i < G:
                        pool.wait_ge(logs_sb, g * G + i + 1)
                        g_.tensor_tensor(bq[:, i], bn[:, i], bd[:, i], ALU.subtract).then_inc(qp_ready, 1)
                        pool.wait_ge(qp_ready, g * 2 * G + 2 * i + 1)
                        g_.tensor_tensor(bn[:, i], bn[:, i], bd[:, i], ALU.add).then_inc(qp_ready, 1)
                    if i >= 2:
                        j = i - 2
                        pool.wait_ge(log1_sb, g * G + j + 1)
                        g_.tensor_tensor(bd[:, j], bd[:, j], bb[:, j], ALU.subtract).then_inc(diff_ready, 1)
                for i in range(G):
                    pool.wait_ge(sig_sb, g * G + i + 1)
                    g_.tensor_tensor(bz[:, i], bz[:, i], adjT[:, i], ALU.mult).then_inc(att_ready, 1)

        @block.scalar
        def _(act):
            s_ = nc.scalar

            def std(g, layer):
                act.wait_ge(var_ready, g * LAYERS + layer + 1)
                s_.activation(stat[:, 2, :], stat[:, 1, :], ACT.Sqrt).then_inc(std_ready, 1)

            act.wait_ge(const_loaded, 16 * 16)
            act.wait_ge(mask_T, 1)
            s_.copy(mask_col[:, :, :], ps[:, 0, 0:B * HALVES].rearrange("p (g t) -> p g t", g=NG)
                    ).then_inc(const_cast, 1)
            with act.Fori(0, NG) as g:
                for b in range(G):
                    act.wait_ge(adjT_ps, g * G + b + 2)
                    if b == 0:
                        act.wait_ge(att_ready, g * G + 1)
                    s_.copy(adjT[:, b], ps[:, b, :].rearrange("p (a n) -> p a n", a=HALVES)).then_inc(adjT_sb, 1)
                std(g, 0)
                act.wait_ge(cnt_ps, g + 1)
                s_.copy(cnt[:, :, :], ps[:, 0:4, :].rearrange("p a (b n) -> p (a b) n", n=N)).then_inc(cnt_sb, 1)
                for b in range(G):
                    r = b % 2
                    act.wait_ge(feat0_ps, g * G + b + 1)
                    s_.copy(feat[:, r], ps[0:F, r, :].rearrange("p (a n) -> p a n", a=2)).then_inc(feat0_sb, 1)
                    act.wait_ge(pre0_ps, g * G + b + 1)
                    s_.activation(tanh_t[:, r, :], ps[0:F, 2 + r, 0:N], ACT.Tanh, bias=bias0[:, :]
                                  ).then_inc(tanh_sb, 1)
                std(g, 1)
                for k in range(K1):
                    q = 2 * (k % 4)
                    act.wait_ge(fetched1_ps, g * K1 + k + 1)
                    s_.copy(scr[:, k, :].rearrange("p (a n) -> p a n", a=2), ps[:, q:q + 2, :]
                            ).then_inc(fetched1_sb, 1)
                for b in range(G):
                    r = b % 2
                    act.wait_ge(aggT_ps, g * G + b + 1)
                    s_.copy(feat[:, r, 0, :], ps[0:F, r, 0:N]).then_inc(aggT_sb, 1)
                    act.wait_ge(hid_ps, g * G + b + 1)
                    s_.activation(hid[:, r, :], ps[:, 2 + r, 0:N], ACT.Relu, bias=bias1[:, :]).then_inc(hid_sb, 1)
                std(g, 2)
                for b in range(G):
                    r = b % 2
                    act.wait_ge(h2T_ps, g * G + b + 1)
                    s_.copy(feat[:, r, 0, :], ps[0:F, r, 0:N]).then_inc(h2T_sb, 1)
                    act.wait_ge(uv_ps, g * G + b + 1)
                    q = 2 + 2 * r
                    s_.copy(u2[:, 2 * b:2 * b + 2, :], ps[:, q:q + 2, 0:H2]).then_inc(uv_sb, 1)
                    s_.copy(v2[:, 2 * b:2 * b + 2, :], ps[:, q:q + 2, H2:2 * H2]).then_inc(uv_sb, 1)
                for b in range(G):
                    r = b % 2
                    act.wait_ge(acc2T_ps, g * G + b + 1)
                    s_.copy(acc2T[:, r, :], ps[0:H2 // 2, r, :]).then_inc(acc2T_sb, 1)
                std(g, 3)
                act.wait_ge(small_ready, g * SMALL + 1)
                s_.activation(sm[:, NORM, :], sm[:, X2, :], ACT.Sqrt).then_inc(small_done, 1)
                act.wait_ge(small_ready, g * SMALL + 2)
                s_.activation(sm[:, S0, :], sm[:, S2, :], ACT.Ln, bias=1.0)
                s_.activation(sm[:, S1, :], sm[:, S2, :], ACT.Ln, scale=-1.0, bias=1.0).then_inc(small_done, 1)
                act.wait_ge(cT_ps, g + 1)
                s_.copy(cT[:, :], ps[0:T, 6, 0:P]).then_inc(cT_sb, 1)
                act.wait_ge(cb_ps, g + 1)
                s_.copy(cb[:, :, :], ps[:, 0:4, :].rearrange("p a (b n) -> p (a b) n", n=N)).then_inc(cb_sb, 1)
                for i in range(G + 2):
                    if i < G:
                        act.wait_ge(LR_ps, g * G + i + 1)
                        s_.copy(LR[:, i % 2], ps[0:FX, 6:8, :].rearrange("p a (b n) -> p (a b) n", n=N)
                                ).then_inc(LR_sb, 1)
                        act.wait_ge(pair_ps, g * G + i + 1)
                        q = 3 * (i % 2) + 2
                        s_.copy(bz[:, i], ps[:, q, :].rearrange("p (a n) -> p a n", a=HALVES)).then_inc(hz_sb, 1)
                        act.wait_ge(clamped, g * G + i + 1)
                        s_.activation(bn[:, i], bn[:, i], ACT.Ln)
                        s_.activation(bd[:, i], bd[:, i], ACT.Ln).then_inc(logs_sb, 1)
                    if 1 <= i <= G:
                        j = i - 1
                        act.wait_ge(qp_ready, g * 2 * G + 2 * j + 2)
                        s_.activation(bq[:, j], bq[:, j], ACT.Exp, scale=0.5)
                        s_.activation(bn[:, j], bn[:, j], ACT.Exp, scale=-0.5).then_inc(exps_sb, 1)
                    if i >= 2:
                        j = i - 2
                        act.wait_ge(s_clipped, g * G + j + 1)
                        s_.activation(bd[:, j], bq[:, j], ACT.Ln, bias=1.0)
                        s_.activation(bb[:, j], bq[:, j], ACT.Ln, scale=-1.0, bias=1.0).then_inc(log1_sb, 1)
                for i in range(G):
                    act.wait_ge(z_ready, g * G + i + 1)
                    s_.activation(bz[:, i], bz[:, i], ACT.Sigmoid).then_inc(sig_sb, 1)
                act.wait_ge(support_ps, g + 1)
                s_.copy(sp[:, :, :].rearrange("p (a b) c -> p a b c", a=4),
                        ps[:, 0:4, :].rearrange("p a (b c) -> p a b c", b=4)[:, :, :, 0:F + 1]
                        ).then_inc(support_sb, 1)
                for n, (dst, src, func) in enumerate(((S1, S0, ACT.Sqrt), (S3, S2, ACT.Tanh), (S1, S0, ACT.Sqrt))):
                    act.wait_ge(small_ready, g * SMALL + 3 + n)
                    s_.activation(sm[:, dst, :], sm[:, src, :], func).then_inc(small_done, 1)
                act.wait_ge(out_ready, g + 1)
                act.dma_start(out.rearrange("(g b) (t p) c -> p g (b t) c", g=NG, p=P)[:, bass.ds(g, 1)]
                              .rearrange("p o t c -> p (o t) c"), xs[:, :, :]).then_inc(out_stored, 16)
            act.wait_ge(out_stored, NG * 16 + 16)

        @block.vector
        def _(dve):
            v_ = nc.vector
            settle = v_.drain

            def per_node(stat_row, width=F):
                return stat_row.unsqueeze(2).broadcast_to([P, T, width])

            def over_halves(rows):
                return rows.unsqueeze(2).broadcast_to(PAIR)

            def flat(t):
                return t.rearrange("p a b n -> p (a b n)")

            banks = ps[:, :, :].rearrange("p g (a n) -> p g a n", a=HALVES)
            node_ps = ps[:, 4:6, :].rearrange("p a (b c) -> p (a b) c", c=F)

            def layernorm_relu(g, layer, src):
                v_.reduce_sum(stat[:, 0, :], src, AX.X)
                settle()
                v_.tensor_scalar(stat[:, 0, :], stat[:, 0, :], -1.0 / F, None, ALU.mult)
                settle()
                v_.tensor_tensor(xc, src, per_node(stat[:, 0, :]), ALU.add)
                settle()
                v_.tensor_tensor(sq, xc, xc, ALU.mult)
                settle()
                v_.reduce_sum(stat[:, 1, :], sq, AX.X)
                settle()
                v_.tensor_scalar(stat[:, 1, :], stat[:, 1, :], 1.0 / F, EPS, ALU.mult, ALU.add).then_inc(var_ready, 1)
                dve.wait_ge(std_ready, g * LAYERS + layer + 1)
                v_.reciprocal(stat[:, 3, :], stat[:, 2, :])
                settle()
                v_.tensor_tensor(h[:, :, :], xc, per_node(stat[:, 3, :]), ALU.mult)
                settle()
                return v_.tensor_scalar(h[:, :, :], h[:, :, :], 0.0, None, ALU.max)

            def split_in_three(value, parts, rest):
                v_.tensor_copy(parts[0], value)
                settle()
                v_.tensor_tensor(rest, value, parts[0], ALU.subtract)
                settle()
                v_.tensor_copy(parts[1], rest)
                settle()
                return v_.tensor_tensor(parts[2], rest, parts[1], ALU.subtract)

            def general_quantiles(g, agg):
                dve.wait_ge(valid_ps, g * T + 1)
                v_.tensor_scalar(all_place[:, 0:P], ps[:, 4, 0:P], -1.0, None, ALU.add)
                v_.tensor_scalar(all_place[:, P:N], ps[:, 4, 0:P], P - 1.0, None, ALU.add)
                settle()
                with dve.Fori(0, T) as t:
                    dve.wait_ge(valid_ps, g * T + t + 1)
                    v_.tensor_scalar(all_valid, psb[:, 5, 0:N], 0.5, None, ALU.is_gt).then_inc(valid_used, 1)
                    for n, (tau, weight) in enumerate(TAUS):
                        v_.tensor_scalar(over[:, 1:2], sm[:, M1, bass.ds(t, 1)], -(1.0 - tau), None, ALU.mult)
                        settle()
                        v_.tensor_scalar(all_wt, all_place, over[:, 1:2], None, ALU.add)
                        settle()
                        v_.scalar_tensor_tensor(all_wt, all_wt, -1.0, all_wt, ALU.mult, ALU.max)
                        settle()
                        v_.tensor_scalar(all_wt, all_wt, -1.0, 1.0, ALU.mult, ALU.add)
                        settle()
                        dst = all_wt if n else all_w
                        v_.tensor_scalar(dst, all_wt, 0.0, weight, ALU.max, ALU.mult)
                        settle()
                        if n:
                            v_.tensor_tensor(all_w, all_w, all_wt, ALU.add)
                            settle()
                    with dve.Fori(0, F) as c:
                        dve.wait_ge(row_ps, g * (T * F) + t * F + c + 1)
                        v_.tensor_tensor(all_left, ps[:, 3, 0:N], all_valid, ALU.mult).then_inc(row_used, 1)
                        settle()
                        for r in range(0, N, 8):
                            v_.max(all_sorted[:, r:r + 8], all_left)
                            settle()
                            v_.match_replace(all_left, all_sorted[:, r:r + 8], all_left, -1.0)
                            settle()
                        v_.tensor_tensor(all_prod, all_sorted, all_w, ALU.mult)
                        settle()
                        v_.reduce_sum(all_agg[:, bass.ds(t, 1), bass.ds(c, 1)].rearrange("p a b -> p (a b)"), all_prod,
                                      AX.X)
                        settle()
                v_.tensor_tensor(agg, all_agg, h[:, :, :], ALU.add)

            def general_relu_sum(g):
                more = N - K2
                settle()
                v_.tensor_scalar(acc2_rest, u2, 0.0, -float(more), ALU.max, ALU.mult)
                settle()
                v_.tensor_tensor(acc2, acc2, acc2_rest, ALU.add)
                for p in range(PAIRS):
                    v_.memset(over[:, 1:2], float(K2 + 1))
                    settle()
                    with dve.Fori(0, more) as k:
                        v_.tensor_scalar(pick2[:, 0], slot2[:, 2 * p:2 * p + 2].rearrange("p a b n -> p (a b n)"),
                                         over[:, 1:2], None, ALU.is_equal).then_inc(more_picked, 1)
                        dve.wait_ge(more_ps, g * (PAIRS * more) + k + (p * more + 1))
                        v_.tensor_tensor(t2[:, 0].rearrange("p (a b) c -> p a (b c)", a=2),
                                         u2[:, 4 * p:4 * p + 4, :].rearrange("p (a b) c -> p a (b c)", a=2),
                                         ps[:, 0:2, 0:2 * H2], ALU.subtract)
                        v_.tensor_scalar(over[:, 1:2], over[:, 1:2], 1.0, None, ALU.add)
                        settle()
                        a2 = acc2[:, 4 * p:4 * p + 4, :].rearrange("p a c -> p (a c)")
                        v_.scalar_tensor_tensor(a2, t2[:, 0].rearrange("p a c -> p (a c)"), 0.0, a2,
                                                ALU.max, ALU.add).then_inc(more_summed, 1)
                        settle()

            dve.wait_ge(const_loaded, 16 * 16)
            v_.tensor_copy(mask_f[:, :], mask_in[:, :]).then_inc(mask_cast, 1)
            v_.tensor_tensor(wsum_2[:, :], w1_2[:, 0, :], w1_2[:, 1, :], ALU.add).then_inc(mask_cast, 1)
            dve.wait_ge(const_made, 13)
            v_.tensor_copy(place[:, :], place_i[:, :])
            dve.wait_ge(const_cast, 1)

            with dve.Fori(0, NG) as g:
                dve.wait_ge(adjT_sb, g * G + G)
                v_.tensor_scalar(any_m, adjT[:, :, :, :], 0.0, None, ALU.is_gt)
                settle()
                for b in range(G):
                    last = v_.tensor_tensor(nb_m[:, b], any_m[:, b], noteye[:, :, :], ALU.mult)
                last.then_inc(nb_ready, 1)
                dve.wait_ge(x_loaded, g * 16 + 16)
                dve.wait_ge(mrow_loaded, g * 16 + 16)
                layernorm_relu(g, 0, x_in[:, :, :]).then_inc(h0_ready, 1)
                dve.wait_ge(cnt_sb, g + 1)
                v_.tensor_scalar(rank1, cnt, 0.5, 0.25, ALU.mult, ALU.add)
                v_.scalar_tensor_tensor(on.rearrange("p a n -> p (a n)"), cnt.rearrange("p a n -> p (a n)"),
                                        DILATE_OVER, mask_row8[:, :], ALU.is_gt, ALU.mult)
                settle()
                v_.tensor_scalar(rank1, rank1, ROUND, None, ALU.add)
                settle()
                v_.tensor_scalar(rank1, rank1, ROUND, None, ALU.subtract)
                settle()
                v_.scalar_tensor_tensor(rank1.rearrange("p a n -> p (a n)"), rank1.rearrange("p a n -> p (a n)"),
                                        FAR, on.rearrange("p a n -> p (a n)"), ALU.subtract, ALU.mult)
                settle()
                v_.tensor_scalar(rank2, rank1, 2.0, 2 * FAR, ALU.mult, ALU.add)
                settle()
                v_.tensor_scalar(rank1, rank1, FAR, None, ALU.add)
                settle()
                dve.wait_ge(nbcum_ps, g + 1)
                v_.tensor_tensor(at1, banks, over_halves(rank1), ALU.is_equal)
                v_.tensor_tensor(at2, banks, over_halves(rank2), ALU.is_equal)
                settle()
                v_.tensor_tensor(at1, at1, at2, ALU.add)
                settle()
                v_.tensor_tensor(gone, at1, nb_m, ALU.mult).then_inc(gone_ready, 1)
                dve.wait_ge(goneT_ps, g + 1)
                v_.tensor_tensor(at1.rearrange("p g a n -> p g (a n)"), gone.rearrange("p g a n -> p g (a n)"),
                                 psb[:, :, 0:HALVES * N], ALU.add)
                settle()
                v_.scalar_tensor_tensor(flat(val_m), flat(at1), 0.5, flat(nb_m), ALU.is_lt, ALU.mult)
                settle()
                for b in range(G):
                    last = v_.tensor_tensor(val_m[:, b], val_m[:, b], eye[:, :, :], ALU.add)
                last.then_inc(val_ready, 1)
                dve.wait_ge(cum1_ps, g + 1)
                v_.tensor_tensor(slot1[:, :, :, :], banks, val_m, ALU.mult).then_inc(slot1_ready, 1)
                dve.wait_ge(cum2_ps, g + 1)
                v_.tensor_tensor(slot2[:, :, :, :], banks, any_m, ALU.mult).then_inc(slot2_ready, 1)
                dve.wait_ge(deg_ps, g + 1)
                v_.tensor_copy(degs[:, :, :], ps[:, 7, 0:2 * T].rearrange("p (a t) -> p a t", a=2))
                v_.tensor_copy(sm[:, MC, :], mask_col[:, bass.ds(g, 1), :].rearrange("p o t -> p (o t)"))

                v_.tensor_scalar(sm[:, S0, :], ps[:, 7, 0:T], -float(K1), None, ALU.add)
                v_.tensor_scalar(sm[:, S1, :], ps[:, 7, T:2 * T], -float(K2), None, ALU.add)
                settle()
                v_.tensor_tensor(sm[:, S0, :], sm[:, S0, :], sm[:, S1, :], ALU.max)
                settle()
                v_.reduce_max(over[:, 0:1], sm[:, S0, :], AX.X).then_inc(over_ready, 1)
                dve.wait_ge(over_ps, g + 1)
                v_.reduce_max(over[0:1, 1:2], ps[0:1, 6, 0:P], AX.X)
                settle()
                v_.tensor_scalar(is_long[:, :], over[0:1, 1:2], 0.0, None, ALU.is_gt).then_inc(long_ready, 1)
                dve.wait_ge(long_ready, g + 1)
                dve.nop(nofuse=True)
                long_group = dve.value_load(is_long[0:1, 0:1])

                dve.wait_ge(dh0_ps, g * G + G)
                dve.wait_ge(out_stored, g * 16 + 16)
                v_.tensor_tensor(xs[:, :, :], x_in[:, :, :], node_ps, ALU.add).then_inc(x_free, 1)

                settle()
                layernorm_relu(g, 1, xs[:, :, :])
                settle()
                split_in_three(h[:, :, :], [hp[:, :, i, :] for i in range(3)], xc).then_inc(parts1_ready, 1)
                for k in range(K1):
                    if k >= SEL:
                        dve.wait_ge(fetched1_ps, g * K1 + k - SEL + 1)
                    v_.tensor_scalar(pick[:, k % SEL], slot1[:, :, :, :], float(k + 1), None, ALU.is_equal
                                     ).then_inc(pick1_ready, 1)
                v_.tensor_scalar(sm[:, M1, :], degs[:, 0, :], -1.0, None, ALU.add)
                settle()
                for n, (tau, weight) in enumerate(TAUS):
                    v_.tensor_scalar(sm[:, S0, :], sm[:, M1, :], -(1.0 - tau), None, ALU.mult)
                    settle()
                    v_.tensor_tensor(wt[:, :, :], place[:, :].unsqueeze(1).broadcast_to([P, T, K1]),
                                     per_node(sm[:, S0, :], K1), ALU.add)
                    settle()
                    wtf = wt[:, :, :].rearrange("p t k -> p (t k)")
                    v_.scalar_tensor_tensor(wtf, wtf, -1.0, wtf, ALU.mult, ALU.max)
                    settle()
                    v_.tensor_scalar(wt[:, :, :], wt[:, :, :], -1.0, 1.0, ALU.mult, ALU.add)
                    settle()
                    if n == 0:
                        v_.tensor_scalar(wq[:, :, :], wt[:, :, :], 0.0, weight, ALU.max, ALU.mult)
                    else:
                        v_.tensor_scalar(wt[:, :, :], wt[:, :, :], 0.0, weight, ALU.max, ALU.mult)
                        settle()
                        v_.tensor_tensor(wq[:, :, :], wq[:, :, :], wt[:, :, :], ALU.add)
                    settle()
                dve.wait_ge(fetched1_sb, g * K1 + K1)
                buf = list(range(K1))
                spare = list(range(K1, NBUF))
                done = 0
                for layer in NETWORK:
                    for at in range(0, len(layer), SPARE // 2):
                        step = layer[at:at + SPARE // 2]
                        if done:
                            dve.wait_ge(sorted_ops, g * SORT_OPS + done)
                        tops = {}
                        for a, b, hi, lo in step:
                            if hi:
                                tops[a] = (spare.pop(0), done + 1)
                                v_.tensor_tensor(scr[:, tops[a][0], :], scr[:, buf[a], :], scr[:, buf[b], :], ALU.max
                                                 ).then_inc(sorted_ops, 1)
                                done += 1
                        for a, b, hi, lo in step:
                            if lo:
                                if hi:
                                    dve.wait_ge(sorted_ops, g * SORT_OPS + tops[a][1])
                                v_.tensor_tensor(scr[:, buf[b], :], scr[:, buf[a], :], scr[:, buf[b], :], ALU.min
                                                 ).then_inc(sorted_ops, 1)
                                done += 1
                        for a, b, hi, lo in step:
                            if hi:
                                spare.append(buf[a])
                                buf[a] = tops[a][0]
                assert done == SORT_OPS
                dve.wait_ge(sorted_ops, g * SORT_OPS + SORT_OPS)
                agg_at, term = spare[0], spare[1:3]
                for d in range(D_USED + 1):
                    if d < D_USED:
                        dst = term[d % 2] if d else agg_at
                        v_.tensor_tensor(scr[:, dst, :].rearrange("p (t c) -> p t c", t=T),
                                         scr[:, buf[d], :].rearrange("p (t c) -> p t c", t=T),
                                         per_node(wq[:, :, d]), ALU.mult)
                    if d >= 2:
                        v_.tensor_tensor(scr[:, agg_at, :], scr[:, agg_at, :], scr[:, term[(d - 1) % 2], :], ALU.add)
                    settle()
                agg = scr[:, AGG, :].rearrange("p (t c) -> p t c", t=T)
                v_.tensor_tensor(agg, scr[:, agg_at, :].rearrange("p (t c) -> p t c", t=T), h[:, :, :], ALU.add)
                settle()
                with dve.If(long_group > 0):
                    general_quantiles(g, agg)
                with dve.Else():
                    dve.sem_inc(valid_used, T)
                    dve.sem_inc(row_used, T * F)
                settle()
                v_.tensor_copy(over[:, 0:1], over[:, 0:1]).then_inc(agg_ready, 1)
                dve.wait_ge(y1_ps, g * G + G)
                v_.tensor_tensor(xc, node_ps, per_node(sm[:, MC, :]), ALU.mult)
                settle()
                v_.tensor_tensor(xs[:, :, :], xs[:, :, :], xc, ALU.add)

                settle()
                layernorm_relu(g, 2, xs[:, :, :]).then_inc(h2_ready, 1)
                v_.tensor_scalar(sm[:, DK, :], degs[:, 1, :], -float(K2), None, ALU.add)
                settle()
                dve.wait_ge(uv_sb, g * 2 * G + 2 * G)
                split_in_three(v2, [vp[:, :, i, :] for i in range(3)], rest2).then_inc(parts2_ready, 1)
                v_.scalar_tensor_tensor(acc2, u2, 0.0, per_node(sm[:, DK, :], H2), ALU.max, ALU.mult)
                n2 = PAIRS * K2
                settle()
                for i in range(n2 + 3):
                    if i < n2:
                        p, k = divmod(i, K2)
                        if i >= PICKS2:
                            dve.wait_ge(fetched2_ps, g * n2 + i - PICKS2 + 1)
                        v_.tensor_scalar(pick2[:, i % PICKS2], slot2[:, 2 * p:2 * p + 2].rearrange("p a b n -> p (a b n)"),
                                         float(k + 1), None, ALU.is_equal).then_inc(pick2_ready, 1)
                    if 2 <= i < n2 + 2:
                        j = i - 2
                        p, q = j // K2, 2 * (j % 4)
                        dve.wait_ge(fetched2_ps, g * n2 + j + 1)
                        if j >= 2:
                            dve.wait_ge(summed2, g * n2 + j - 1)
                        v_.tensor_tensor(t2[:, j % 2].rearrange("p (a b) c -> p a (b c)", a=2),
                                         u2[:, 4 * p:4 * p + 4, :].rearrange("p (a b) c -> p a (b c)", a=2),
                                         ps[:, q:q + 2, 0:2 * H2], ALU.subtract).then_inc(taken2, 1)
                    if i >= 3:
                        j = i - 3
                        p = j // K2
                        dve.wait_ge(taken2, g * n2 + j + 1)
                        if j >= 1:
                            dve.wait_ge(summed2, g * n2 + j)
                        a2 = acc2[:, 4 * p:4 * p + 4, :].rearrange("p a c -> p (a c)")
                        v_.scalar_tensor_tensor(a2, t2[:, j % 2].rearrange("p a c -> p (a c)"), 0.0, a2,
                                                ALU.max, ALU.add).then_inc(summed2, 1)
                with dve.If(long_group > 0):
                    general_relu_sum(g)
                with dve.Else():
                    dve.sem_inc(more_picked, PAIRS * (N - K2))
                    dve.sem_inc(more_summed, PAIRS * (N - K2))
                v_.tensor_tensor(xc, per_node(degs[:, 1, :]), b2_all[:, :].unsqueeze(1).broadcast_to([P, T, F]),
                                 ALU.mult)
                settle()
                v_.tensor_tensor(xs[:, :, :], xs[:, :, :], xc, ALU.add)
                settle()
                dve.wait_ge(y2_ps, g * G + G)
                v_.tensor_tensor(xs[:, :, :], xs[:, :, :], node_ps, ALU.add)

                settle()
                layernorm_relu(g, 3, xs[:, :, :])
                settle()

                def row(i):
                    return sm[:, i, :]

                def dot_with(dst, a, b):
                    v_.tensor_tensor(sq, a, b, ALU.mult)
                    settle()
                    v_.reduce_sum(dst, sq, AX.X)
                    settle()

                def ts(dst, src, s1, s2, op0, op1=ALU.bypass):
                    i = v_.tensor_scalar(row(dst), row(src), s1, s2, op0, op1) if s2 is not None else \
                        v_.tensor_scalar(row(dst), row(src), s1, None, op0)
                    settle()
                    return i

                def tt(dst, a, b, op):
                    i = v_.tensor_tensor(row(dst), row(a), row(b), op)
                    settle()
                    return i

                hh = h[:, :, :]
                dot_with(row(X2), hh, hh)
                v_.tensor_copy(row(M1), row(X2)).then_inc(small_ready, 1)
                dot_with(row(WS), hh, att_w[:, 0, :].unsqueeze(1).broadcast_to([P, T, F]))
                dot_with(row(WL), hh, att_w[:, 1, :].unsqueeze(1).broadcast_to([P, T, F]))
                ts(BM, X2, -1.0, 1.0, ALU.mult, ALU.add)
                ts(LAM, BM, MIN_NORM, None, ALU.max)
                tt(LB, LAM, BM, ALU.mult)
                tt(LW, LAM, WL, ALU.mult)
                ts(NLW, LW, -1.0, None, ALU.mult)
                ts(S0, X2, -2.0, 1.0, ALU.mult, ALU.add)
                tt(S1, S0, X2, ALU.add)
                tt(DF, BM, S1, ALU.subtract)
                tt(S1, X2, X2, ALU.mult)
                tt(DD, S0, S1, ALU.add)
                ts(DD, DD, MIN_NORM, None, ALU.max)
                v_.reciprocal(row(S3), row(DD))
                settle()
                tt(DF, DF, S3, ALU.mult)
                v_.scalar_tensor_tensor(row(S4), row(DF), -1.0, row(DF), ALU.mult, ALU.max)
                settle()
                dve.wait_ge(small_done, g * SMALL + 1)
                tt(SN, S4, NORM, ALU.mult)
                ts(SN, SN, MIN_NORM, None, ALU.max)
                v_.tensor_scalar(row(S2), row(SN), CLIP, None, ALU.min).then_inc(small_ready, 1)
                v_.reciprocal(row(S4), row(SN))
                settle()
                tt(S4, S4, DF, ALU.mult)
                tt(S4, S4, LAM, ALU.mult)
                tt(S4, S4, WS, ALU.mult)
                dve.wait_ge(small_done, g * SMALL + 2)
                tt(S0, S0, S1, ALU.subtract)
                tt(S0, S0, S4, ALU.mult)
                v_.tensor_scalar(row(CC), row(S0), 0.5, att_c[:, 0:1], ALU.mult, ALU.add)
                v_.tensor_copy(tok[:, 0, :, 0:F], hh)
                v_.tensor_scalar(tok[:, 1, :, 0:F], hh, -2.0, None, ALU.mult)
                v_.tensor_scalar(tok[:, 2, :, 0:F], hh, -2.0, None, ALU.mult)
                v_.scalar_tensor_tensor(tok[:, 3, :, 0:F], hh, 2.0, per_node(row(LW)), ALU.mult, ALU.mult)
                for which, rows in enumerate(((X2, None, WL), (X2, None, 0.0), (None, X2, 0.0), (NLW, NLW, LB))):
                    for c, r in enumerate(rows):
                        dst = tok[:, which, :, F + c]
                        if r is None or r == 0.0 and isinstance(r, float):
                            v_.memset(dst, 1.0 if r is None else 0.0)
                        else:
                            v_.tensor_copy(dst, row(r))
                settle()
                v_.tensor_copy(row(M1), row(CC)).then_inc(tok_ready, 1)

                for i in range(G + 1):
                    if i < G:
                        q = 3 * (i % 2)
                        dve.wait_ge(pair_ps, g * G + i + 1)
                        v_.tensor_scalar(bd[:, i], banks[:, q], MIN_NORM, None, ALU.max)
                        v_.tensor_scalar(bn[:, i], banks[:, q + 1], MIN_SQ, None, ALU.max).then_inc(clamped, 1)
                    if i >= 1:
                        j = i - 1
                        dve.wait_ge(exps_sb, g * G + j + 1)
                        v_.tensor_scalar(bq[:, j], bq[:, j], CLIP, None, ALU.min).then_inc(s_clipped, 1)
                dve.wait_ge(cb_sb, g + 1)
                dve.wait_ge(hz_sb, g * G + G)
                for i in range(G + 2):
                    if i < G:
                        dve.wait_ge(diff_ready, g * G + i + 1)
                        v_.scalar_tensor_tensor(f2(bd[:, i]), f2(bd[:, i]), 0.5, f2(bn[:, i]), ALU.mult, ALU.mult)
                    if 1 <= i <= G:
                        v_.tensor_tensor(bz[:, i - 1], bz[:, i - 1], bd[:, i - 1], ALU.mult)
                    if i >= 2:
                        v_.tensor_tensor(bz[:, i - 2], bz[:, i - 2],
                                         cb[:, i - 2].unsqueeze(1).broadcast_to([P, HALVES, N]), ALU.add
                                         ).then_inc(z_ready, 1)
                    settle()
                v_.tensor_copy(feat3[:, :, 0:F], hh)
                v_.tensor_scalar(feat3[:, :, F], row(X2), 1.0, None, ALU.add).then_inc(feat3_ready, 1)
                for i in range(G):
                    dve.wait_ge(att_ready, g * G + i + 2)
                    v_.tensor_tensor(bd[:, i], bd[:, i], bz[:, i], ALU.mult).then_inc(weight_ready, 1)

                dve.wait_ge(support_sb, g + 2)
                s1 = sp[:, :, 0:F]
                dot_with(row(S0), hh, s1)
                v_.scalar_tensor_tensor(row(S1), row(S0), -2.0, sp[:, :, F], ALU.mult, ALU.add)
                settle()
                tt(S1, S1, LAM, ALU.mult)
                v_.tensor_tensor(y3, s1, per_node(row(LB)), ALU.mult)
                v_.tensor_tensor(z3, hh, per_node(row(S1)), ALU.mult)
                settle()
                v_.tensor_tensor(y3, y3, z3, ALU.subtract)
                settle()
                v_.tensor_scalar(y3, y3, CLAMP, -CLAMP, ALU.min, ALU.max)
                settle()
                dot_with(row(S0), y3, y3)
                v_.tensor_scalar(row(S0), row(S0), MIN_NORM * MIN_NORM, None, ALU.max).then_inc(small_ready, 1)
                v_.reciprocal(row(S4), row(LAM))
                settle()
                dve.wait_ge(small_done, g * SMALL + 3)
                v_.tensor_tensor(row(S2), row(S1), row(S4), ALU.mult).then_inc(small_ready, 1)
                v_.reciprocal(row(S5), row(S1))
                settle()
                dve.wait_ge(small_done, g * SMALL + 4)
                tt(S5, S5, S3, ALU.mult)
                v_.tensor_tensor(y3, y3, per_node(row(S5)), ALU.mult)
                settle()
                dot_with(row(S2), y3, y3)
                dot_with(row(S3), hh, y3)
                ts(S4, S3, 2.0, 1.0, ALU.mult, ALU.add)
                tt(S5, S4, S2, ALU.add)
                tt(S2, S2, X2, ALU.mult)
                tt(S4, S4, S2, ALU.add)
                ts(S4, S4, MIN_NORM, None, ALU.max)
                v_.reciprocal(row(S3), row(S4))
                settle()
                tt(S5, S5, S3, ALU.mult)
                tt(S4, BM, S3, ALU.mult)
                v_.tensor_tensor(z3, hh, per_node(row(S5)), ALU.mult)
                v_.tensor_tensor(y3, y3, per_node(row(S4)), ALU.mult)
                settle()
                v_.tensor_tensor(y3, y3, z3, ALU.add)
                settle()
                dot_with(row(S0), y3, y3)
                v_.tensor_scalar(row(S0), row(S0), MIN_NORM * MIN_NORM, None, ALU.max).then_inc(small_ready, 1)
                dve.wait_ge(small_done, g * SMALL + 5)
                v_.reciprocal(row(S2), row(S1))
                settle()
                ts(S2, S2, MAXNORM, 1.0, ALU.mult, ALU.min)
                v_.tensor_tensor(y3, y3, per_node(row(S2)), ALU.mult)
                settle()
                v_.tensor_tensor(xs[:, :, :], xs[:, :, :], y3, ALU.add).then_inc(out_ready, 1)

        @block.tensor
        def _(pe):
            t_ = nc.tensor

            def mm(o, lhsT, rhs, start=True, stop=True):
                return t_.matmul(o, lhsT, rhs, start=start, stop=stop)

            def held():
                pe.nop(nofuse=True)

            def half(a):
                return slice(a * P, (a + 1) * P)

            def running_count(mask):
                for b in range(G):
                    mm(ps[:, b, 0:N], tri[:, :], mask[:, b, 0, :])
                    mm(ps[:, b, N:2 * N], onesb[:, :], mask[:, b, 0, :], stop=False)
                    last = mm(ps[:, b, N:2 * N], tri[:, :], mask[:, b, 1, :], start=False)
                return last

            def node_out(b, a, terms):
                o = ps[:, 4 + b // 4, (b % 4) * P + a * F:(b % 4) * P + (a + 1) * F]
                for n, (l, r) in enumerate(terms):
                    last = mm(o, l, r, start=n == 0, stop=n == len(terms) - 1)
                return last

            def general_rows(g):
                pe.wait_ge(sorted_ops, g * SORT_OPS + SORT_OPS)
                mm(ps[:, 4, 0:P], onesb[:, :], tri[:, :])
                for b in range(G):
                    for a in range(HALVES):
                        t = 2 * b + a
                        if t >= 1:
                            pe.wait_ge(valid_used, g * T + t)
                            held()
                        for c in range(HALVES):
                            last = t_.transpose(psb[:, 5, half(c)], slot1[:, b, c, half(a)], identb[:, :])
                        last.then_inc(valid_ps, 1)
                        with pe.Fori(0, F) as c:
                            pe.wait_ge(row_used, g * (T * F) + c + (t * F + 1))
                            for j in range(HALVES):
                                for part in range(3):
                                    last = mm(ps[:, 3, half(j)],
                                              hp[:, 2 * b + j, part, bass.ds(c, 1)].broadcast_to([P, P]), identb[:, :],
                                              start=part == 0, stop=part == 2)
                            last.then_inc(row_ps, 1)

            def general_fetch(g):
                more = N - K2
                for p in range(PAIRS):
                    with pe.Fori(0, more) as k:
                        pe.wait_ge(more_picked, g * (PAIRS * more) + k + (p * more + 1))
                        for t in range(4):
                            b, a = divmod(t, 2)
                            for c in range(HALVES):
                                for part in range(3):
                                    at = (b * HALVES + c) * N + a * P
                                    last = mm(ps[:, b, a * H2:(a + 1) * H2], pick2[:, 0, at:at + P],
                                              vp[:, 4 * p + 2 * b + c, part, :],
                                              start=c == 0 and part == 0, stop=c == 1 and part == 2)
                        last.then_inc(more_ps, 1)

            pe.wait_ge(const_loaded, 16 * 16)
            pe.wait_ge(const_made, 13)
            pe.wait_ge(mask_cast, 2)
            t_.transpose(ps[:, 0, 0:B * HALVES], mask_f[:, :], identf[0:B * HALVES, 0:B * HALVES]).then_inc(mask_T, 1)
            pe.wait_ge(const_cast, 1)
            one_row = onesf[0:1, :]
            with pe.Fori(0, NG) as g:
                pe.wait_ge(support_sb, g + 1)
                for b in range(G):
                    if b % (G // 2) == 0:
                        pe.wait_ge(adj_loaded, g * 16 * G + 16 * (b + G // 2))
                    held()
                    for a in range(HALVES):
                        for c in range(HALVES):
                            last = t_.transpose(ps[:, b, c * N + a * P:c * N + (a + 1) * P],
                                                adj_in[:, (2 * b + a) % (T // 2), half(c)], identf[:, :])
                    last.then_inc(adjT_ps, 1)
                pe.wait_ge(nb_ready, g + 1)
                for b in range(G):
                    o = ps[:, b // 2, (b % 2) * N:(b % 2 + 1) * N]
                    mm(o, onesb[:, :], nb_m[:, b, 0, :], stop=False)
                    last = mm(o, onesb[:, :], nb_m[:, b, 1, :], start=False)
                last.then_inc(cnt_ps, 1)
                pe.wait_ge(cnt_sb, g + 1)
                running_count(nb_m).then_inc(nbcum_ps, 1)
                pe.wait_ge(gone_ready, g + 1)
                held()
                for b in range(G):
                    for a in range(HALVES):
                        for c in range(HALVES):
                            last = t_.transpose(psb[:, b, c * N + a * P:c * N + (a + 1) * P],
                                                gone[:, b, a, half(c)], identb[:, :])
                last.then_inc(goneT_ps, 1)
                pe.wait_ge(val_ready, g + 1)
                running_count(val_m).then_inc(cum1_ps, 1)
                pe.wait_ge(slot1_ready, g + 1)
                running_count(any_m).then_inc(cum2_ps, 1)
                pe.wait_ge(slot2_ready, g + 1)
                for n, mask in enumerate((val_m, any_m)):
                    for b in range(G):
                        for a in range(HALVES):
                            at = n * T + 2 * b + a
                            mm(ps[:, 7, at:at + 1], mask[:, b, 0, half(a)], onesb[:, 0:1], stop=False)
                            last = mm(ps[:, 7, at:at + 1], mask[:, b, 1, half(a)], onesb[:, 0:1], start=False)
                last.then_inc(deg_ps, 1)
                pe.wait_ge(over_ready, g + 1)
                held()
                t_.transpose(ps[0:1, 6, 0:P], over[:, 0:1], identf[:, :]).then_inc(over_ps, 1)
                pe.wait_ge(long_ready, g + 1)
                held()
                long_group = pe.value_load(is_long[0:1, 0:1])

                pe.wait_ge(h0_ready, g + 1)
                for b in range(G):
                    r = b % 2
                    held()
                    mm(ps[0:F, r, N:2 * N], h[:, 2 * b, :], adjT[:, b, 0, :], stop=False)
                    mm(ps[0:F, r, N:2 * N], h[:, 2 * b + 1, :], adjT[:, b, 1, :], start=False)
                    for a in range(HALVES):
                        last = t_.transpose(ps[0:F, r, half(a)], h[:, 2 * b + a, :], identf[:, :])
                    last.then_inc(feat0_ps, 1)
                    pe.wait_ge(feat0_sb, g * G + b + 1)
                    held()
                    mm(ps[0:F, 2 + r, 0:N], w1_0[:, 0, :], feat[:, r, 0, :], stop=False)
                    mm(ps[0:F, 2 + r, 0:N], w1_0[:, 1, :], feat[:, r, 1, :], start=False).then_inc(pre0_ps, 1)
                    pe.wait_ge(tanh_sb, g * G + b + 1)
                    held()
                    for a in range(HALVES):
                        last = node_out(b, a, [(tanh_t[:, r, half(a)], w2_0[:, :]), (one_row, brow[:, 0, :])])
                    last.then_inc(dh0_ps, 1)

                pe.wait_ge(parts1_ready, g + 1)
                for k in range(K1):
                    pe.wait_ge(pick1_ready, g * K1 + k + 1)
                    if k >= 4:
                        pe.wait_ge(fetched1_sb, g * K1 + k - 3)
                    for t in range(T):
                        b, a = divmod(t, 2)
                        o = ps[:, 2 * (k % 4) + t // 8, (t % 8) * F:(t % 8 + 1) * F]
                        for c in range(HALVES):
                            for part in range(3):
                                last = mm(o, pick[:, k % SEL, b, c, half(a)], hp[:, 2 * b + c, part, :],
                                          start=c == 0 and part == 0, stop=c == 1 and part == 2)
                    last.then_inc(fetched1_ps, 1)
                with pe.If(long_group > 0):
                    general_rows(g)
                with pe.Else():
                    pe.sem_inc(valid_ps, T)
                    pe.sem_inc(row_ps, T * F)
                pe.wait_ge(agg_ready, g + 1)
                for b in range(G):
                    r = b % 2
                    held()
                    for a in range(HALVES):
                        t = 2 * b + a
                        last = t_.transpose(ps[0:F, r, half(a)], scr[:, AGG, t * F:(t + 1) * F], identf[:, :])
                    last.then_inc(aggT_ps, 1)
                    pe.wait_ge(aggT_sb, g * G + b + 1)
                    held()
                    mm(ps[:, 2 + r, 0:N], w1_1[:, :], feat[:, r, 0, :]).then_inc(hid_ps, 1)
                    pe.wait_ge(hid_sb, g * G + b + 1)
                    held()
                    for a in range(HALVES):
                        last = node_out(b, a, [(hid[:, r, half(a)], w2_1[:, :]), (one_row, brow[:, 1, :])])
                    last.then_inc(y1_ps, 1)

                pe.wait_ge(h2_ready, g + 1)
                for b in range(G):
                    r = b % 2
                    held()
                    for a in range(HALVES):
                        last = t_.transpose(ps[0:F, r, half(a)], h[:, 2 * b + a, :], identf[:, :])
                    last.then_inc(h2T_ps, 1)
                    pe.wait_ge(h2T_sb, g * G + b + 1)
                    if b >= 2:
                        pe.wait_ge(uv_sb, g * 2 * G + 2 * (b - 1))
                    held()
                    for a in range(HALVES):
                        q = 2 + 2 * r + a
                        mm(ps[:, q, 0:H2], feat[:, r, 0, half(a)], wsum_2[:, :], stop=False)
                        mm(ps[:, q, 0:H2], one_row, brow2[:, :], start=False)
                        last = mm(ps[:, q, H2:2 * H2], feat[:, r, 0, half(a)], w1_2[:, 1, :])
                    last.then_inc(uv_ps, 1)
                pe.wait_ge(parts2_ready, g + 1)
                n2 = PAIRS * K2
                for i in range(n2):
                    p, k = divmod(i, K2)
                    pe.wait_ge(pick2_ready, g * n2 + i + 1)
                    if i >= 4:
                        pe.wait_ge(taken2, g * n2 + i - 3)
                    for t in range(4):
                        b, a = divmod(t, 2)
                        o = ps[:, 2 * (i % 4) + b, a * H2:(a + 1) * H2]
                        for c in range(HALVES):
                            for part in range(3):
                                at = (b * HALVES + c) * N + a * P
                                last = mm(o, pick2[:, i % PICKS2, at:at + P], vp[:, 4 * p + 2 * b + c, part, :],
                                          start=c == 0 and part == 0, stop=c == 1 and part == 2)
                    last.then_inc(fetched2_ps, 1)
                with pe.If(long_group > 0):
                    general_fetch(g)
                with pe.Else():
                    pe.sem_inc(more_ps, PAIRS * (N - K2))
                pe.wait_ge(summed2, g * n2 + n2)
                pe.wait_ge(more_summed, g * (PAIRS * (N - K2)) + PAIRS * (N - K2))
                for b in range(G):
                    r = b % 2
                    held()
                    for a in range(HALVES):
                        for c in range(2):
                            last = t_.transpose(ps[0:H2 // 2, r, c * N + a * P:c * N + (a + 1) * P],
                                                acc2[:, 2 * b + a, c * (H2 // 2):(c + 1) * (H2 // 2)], identf[:, :])
                    last.then_inc(acc2T_ps, 1)
                    pe.wait_ge(acc2T_sb, g * G + b + 1)
                    held()
                    for a in range(HALVES):
                        last = node_out(b, a, [(acc2T[:, r, c * N + a * P:c * N + (a + 1) * P], w2_2[:, c, :])
                                               for c in range(2)])
                    last.then_inc(y2_ps, 1)

                pe.wait_ge(tok_ready, g + 1)
                held()
                t_.transpose(ps[0:T, 6, 0:P], sm[:, M1, :], identf[:, :]).then_inc(cT_ps, 1)
                pe.wait_ge(cT_sb, g + 1)
                held()
                for t in range(T):
                    b, a = divmod(t, 2)
                    last = mm(ps[:, b // 2, (b % 2) * N + a * P:(b % 2) * N + (a + 1) * P],
                              identf[0:T, t:t + 1].broadcast_to([T, P]), cT[:, :])
                last.then_inc(cb_ps, 1)
                for i in range(G):
                    if i == 0:
                        pe.wait_ge(cb_sb, g + 1)
                    held()
                    for which in range(4):
                        for a in range(HALVES):
                            o = (which % 2) * N + a * P
                            last = t_.transpose(ps[0:FX, 6 + which // 2, o:o + P], tok[:, which, 2 * i + a, :],
                                                identf[:, :])
                    last.then_inc(LR_ps, 1)
                    pe.wait_ge(LR_sb, g * G + i + 1)
                    if i >= 2:
                        pe.wait_ge(clamped, g * G + i - 1)
                        pe.wait_ge(hz_sb, g * G + i - 1)
                    held()
                    for m in range(3):
                        for a in range(HALVES):
                            last = mm(ps[:, 3 * (i % 2) + m, a * N:(a + 1) * N], LR[:, i % 2, 0, half(a)],
                                      LR[:, i % 2, 1 + m, :])
                    last.then_inc(pair_ps, 1)
                pe.wait_ge(feat3_ready, g + 1)
                for b in range(G):
                    pe.wait_ge(weight_ready, g * G + b + 1)
                    held()
                    for a in range(HALVES):
                        t = 2 * b + a
                        o = ps[:, t // 4, (t % 4) * P:(t % 4) * P + F + 1]
                        mm(o, bd[:, b, 0, half(a)], feat3[:, 2 * b, :], stop=False)
                        last = mm(o, bd[:, b, 1, half(a)], feat3[:, 2 * b + 1, :], start=False)
                last.then_inc(support_ps, 1)


def kernel(**inputs):
    import concourse.bacc as bacc
    from concourse.bass_utils import run_bass_kernel_spmd

    nc = bacc.Bacc("TRN2", target_bir_lowering=False, num_devices=1)
    arrays, args = {}, []
    for name in ("x", "adj", "nodemask", "L0_gnn_W1", "L0_gnn_b1", "L0_gnn_W2", "L0_gnn_b2",
                 "L1_gnn_W1", "L1_gnn_b1", "L1_gnn_W2", "L1_gnn_b2", "L2_gnn_W1", "L2_gnn_b1", "L2_gnn_W2",
                 "L2_gnn_b2", "L3_gnn_att_W", "L3_gnn_att_b"):
        a = np.ascontiguousarray(inputs[name])
        if a.dtype == np.bool_:
            a = a.view(np.uint8)
        arrays[f"in_{name}"] = a
        args.append(nc.dram_tensor(f"in_{name}", a.shape, mybir.dt.from_np(a.dtype), kind="ExternalInput").ap())
    args.append(nc.dram_tensor("out", (B, N, F), F32, kind="ExternalOutput").ap())
    program(nc, *args)
    result = run_bass_kernel_spmd(nc, [arrays], core_ids=[0])
    return result.results[0]["out"]
```

```python
import numpy as np
import concourse.bass as bass
import concourse.mybir as mybir
from concourse.alu_op_type import AluOpType as ALU
from contextlib import ExitStack

F32 = mybir.dt.float32
BF16 = mybir.dt.bfloat16
I32 = mybir.dt.int32
U8 = mybir.dt.uint8
ACT = mybir.ActivationFunctionType
AX = mybir.AxisListType

B, N, F = 32, 256, 64
P = 128
HALVES = N // P
G = 4
NG = B // G
T = G * HALVES
Q = 4
R = N // Q
W = G // 2
U = Q * W
H1, H2 = 128, 192
CLASSES = (dict(k=12, tiles=(0, 3 * W)), dict(k=20, tiles=(3 * W, 4 * W)))
K1 = max(c["k"] for c in CLASSES)
K2Q = (8, 10, 12, 22)
UNITS = [(k, q, q + 1 if k >= K2Q[q + 1] else q + 2) if k < K2Q[q] else (k, q + 1, q + 2)
         for k in range(K2Q[-1]) for q in (0, 2) if k < K2Q[q + 1]]
DIRECT = 14
TAUS = [(0.25, 0.25), (0.5, 0.5), (0.75, 0.25)]
DILATE_OVER = 10.0
FAR = 1000.0
ROUND = 8388608.0
EPS = 1e-5
MIN_NORM = 1e-15
MIN_SQ = 1e-18
CLIP = float(np.float32(1.0 - 1e-7))
MAXNORM = 1.0 - 0.004
CLAMP = 1e6
FX = F + 3
SPARE = 6
PICKS1, PICKS2 = 2, 3


def used_places(k):
    return int(np.ceil(0.75 * (k - 1))) + 1


def sorting_steps(n):
    steps = []

    def sort(lo, size):
        if size == 1 or lo >= n:
            return
        p = size // 2
        sort(lo, p)
        sort(lo + p, p)
        k = p
        while k >= 1:
            pairs = [(i + j, i + j + k) for j in range(lo + k % p, lo + size - k, 2 * k)
                     for i in range(min(k, lo + size - j - k))
                     if (i + j) // size == (i + j + k) // size and i + j + k < n]
            steps.extend(pairs[at:at + SPARE // 2] for at in range(0, len(pairs), SPARE // 2))
            k //= 2

    size = 1
    while size < n:
        size *= 2
    sort(0, size)
    needed, kept = set(range(used_places(n))), []
    for step in reversed(steps):
        out = [(a, b, a in needed, b in needed) for a, b in step if a in needed or b in needed]
        for a, b, _, _ in out:
            needed |= {a, b}
        if out:
            kept.append(out)
    return kept[::-1]


for c in CLASSES:
    c["steps"] = sorting_steps(c["k"])
    c["ops"] = sum(hi + lo for step in c["steps"] for _, _, hi, lo in step)
    c["tiles_n"] = c["tiles"][1] - c["tiles"][0]


def program(nc, x, adj, nodemask, W1_0, b1_0, W2_0, b2_0, W1_1, b1_1, W2_1, b2_1, W1_2, b1_2, W2_2, b2_2,
            att_W, att_b, out):
    ctx = ExitStack()
    with ctx:
        def sb(name, shape, dt=F32):
            return ctx.enter_context(nc.sbuf_tensor(name, shape, dt))

        def sem(name):
            return ctx.enter_context(nc.semaphore(name))

        identf = sb("identf", [P, P])
        identb = sb("identb", [P, P], BF16)
        tri = sb("tri", [P, P], BF16)
        onesb = sb("onesb", [P, P], BF16)
        onesf = sb("onesf", [P, P])
        eye = sb("eye", [P, HALVES, N], BF16)
        noteye = sb("noteye", [P, HALVES, N], BF16)
        count_i = sb("count_i", [P, N], I32)
        count_row = sb("count_row", [P, N])
        part_i = sb("part_i", [P, T], I32)
        node_col = sb("node_col", [P, T])
        rank_i = sb("rank_i", [P, U], I32)
        rank_col = sb("rank_col", [P, U])
        caps = sb("caps", [P, 2, U])
        w1_0 = sb("w1_0", [F, 2, F])
        w2_0 = sb("w2_0", [F, F])
        w1_1 = sb("w1_1", [F, H1])
        w2_1 = sb("w2_1", [H1, F])
        w1_2 = sb("w1_2", [F, 2, H2])
        wsum_2 = sb("wsum_2", [F, H2])
        w2_2 = sb("w2_2", [H2 // 2, 2, F])
        bias0 = sb("bias0", [F, 1])
        bias1 = sb("bias1", [H1, 1])
        brow = sb("brow", [1, 2, F])
        brow2 = sb("brow2", [1, H2])
        b2_all = sb("b2_all", [P, F])
        att_w = sb("att_w", [P, 2, F])
        att_c = sb("att_c", [P, 1])
        mask_in = sb("mask_in", [B * HALVES, P], U8)
        mask_f = sb("mask_f", [B * HALVES, P])
        mask_col = sb("mask_col", [P, NG, T])

        adj_in = sb("adj_in", [P, T, N])
        x_in = sb("x_in", [P, T, F])
        slot1 = sb("slot1", [P, G, HALVES, N], BF16)
        perm = sb("perm", [P, G, HALVES, N], BF16)
        permT = sb("permT", [P, Q, W, N], BF16)
        hA = sb("hA", [P, T, F])
        hpA = sb("hpA", [P, T, 3, F], BF16)
        pick1 = sb("pick1", [P, PICKS1, G * HALVES, N], BF16)
        feat = sb("feat", [F, 2, 2, N])
        hid = sb("hid", [P, 2, N])
        tanh_t = hid[0:F, :, :]
        xcA = sb("xcA", [P, T, F])
        sqA = sb("sqA", [P, T, F])
        agg = sb("agg", [P, U, F])
        aggp = sb("aggp", [P, 3, U, F], BF16)
        smA = sb("smA", [P, 20, T])
        wq = sb("wq", [P, U, K1])
        wt = sb("wt", [P, U, K1])
        over = sb("over", [P, 4])
        adjT = [sb(f"adjT{n}", [P, G, HALVES, N]) for n in range(2)]
        slot2 = [sb(f"slot2{n}", [P, G, HALVES, N], BF16) for n in range(2)]
        xs = [sb(f"xs{n}", [P, T, F]) for n in range(2)]
        deg_sorted = [sb(f"deg_sorted{n}", [P, 2, U]) for n in range(2)]
        deg_node = [sb(f"deg_node{n}", [P, T]) for n in range(2)]
        is_long = [sb(f"is_long{n}", [1, 1], I32) for n in range(2)]
        hB = sb("hB", [P, T, F])
        hpB = sb("hpB", [P, T, 3, F], BF16)
        pick2 = sb("pick2", [P, PICKS2, T, 2 * R], BF16)
        featB = sb("featB", [F, 2, 2, N])
        LR = sb("LR", [FX, 4, N])
        cT = sb("cT", [T, P])
        xcB = sb("xcB", [P, T, F])
        sqB = sb("sqB", [P, T, F])
        smB = sb("smB", [P, 28, T])
        overB = sb("overB", [P, 1])

        KB = 1024
        memA = sb("memA", [P, 10 * KB])
        memB = sb("memB", [P, 12 * KB + 96])

        def region(mem, byte, shape, dt=F32):
            n = int(np.prod(shape[1:]))
            v = mem[:, :].bitcast(BF16)[0:shape[0], byte // 2:byte // 2 + n] if dt == BF16 else \
                mem[0:shape[0], byte // 4:byte // 4 + n]
            names = "abcd"[:len(shape) - 1]
            if len(shape) == 2:
                return v
            return v.rearrange(f"p ({' '.join(names)}) -> p {' '.join(names)}",
                               **{c: s for c, s in zip(names, shape[1:])})

        PAIR = [P, G, HALVES, N]
        any_T = region(memA, 0, PAIR, BF16)
        nb_T = region(memA, 4 * KB, PAIR, BF16)
        any_m = region(memA, 8 * KB, PAIR, BF16)
        nb_m = region(memA, 12 * KB, PAIR, BF16)
        key_row = region(memA, 16 * KB, [P, G, N])
        at1 = region(memA, 16 * KB, PAIR, BF16)
        at2 = region(memA, 20 * KB, PAIR, BF16)
        gone = region(memA, 24 * KB, PAIR, BF16)
        val_m = region(memA, 28 * KB, PAIR, BF16)
        less = region(memA, 32 * KB, PAIR, BF16)
        val_s = region(memA, 36 * KB, PAIR, BF16)
        any_s = region(memA, 0, PAIR, BF16)
        byte = 0
        for c in CLASSES:
            c["buf"] = region(memA, byte, [P, c["k"] + SPARE, c["tiles_n"] * F])
            byte += (c["k"] + SPARE) * c["tiles_n"] * F * 4
        assert byte <= 40 * KB
        all_valid = region(memA, 0, [P, N])
        all_left = region(memA, KB, [P, N])
        all_sorted = region(memA, 2 * KB, [P, N])
        all_w = region(memA, 3 * KB, [P, N])
        all_wt = region(memA, 4 * KB, [P, N])
        all_prod = region(memA, 5 * KB, [P, N])
        all_agg = region(memA, 6 * KB, [P, T, F])
        u2 = region(memB, 0, [P, U, H2])
        v2 = region(memB, 6 * KB, [P, T, H2])
        vp = region(memB, 12 * KB, [P, T, 3, H2], BF16)
        acc2 = region(memB, 21 * KB, [P, U, H2])
        up = [region(memB, at * KB, [P, U, H2], BF16) for at in (27, 6, 30)]
        permT2 = region(memB, 33 * KB, [P, Q, W, N], BF16)
        yp = region(memB, 37 * KB, [P, 3, U * F], BF16)
        y_sorted = region(memB, 41 * KB, [P, U, F])
        t2 = region(memB, 37 * KB, [P, 2, 2 * W, H2])
        more_h = region(memB, 41 * KB, [P, H2])
        acc2T = region(memB, 6 * KB, [H2 // 2, 2, 4 * N])
        bn = region(memB, 0, PAIR)
        bd = region(memB, 8 * KB, PAIR)
        bq = region(memB, 16 * KB, PAIR)
        bz = region(memB, 24 * KB, PAIR)
        bb = region(memB, 32 * KB, [P, 2, HALVES, N])
        cb = region(memB, 36 * KB, [P, G, N])
        tok = region(memB, 40 * KB, [P, 4, T, FX])
        feat3 = region(memB, 0, [P, T, F + 1])
        sp = region(memB, 4 * KB, [P, T, F + 1])
        y3 = region(memB, 16 * KB, [P, T, F])
        z3 = region(memB, 18 * KB, [P, T, F])

        ps = ctx.enter_context(nc.psum_tensor("ps", [P, 8, 512], F32))
        psb = ps[:, :, :].bitcast(BF16)

        const_loaded = sem("const_loaded")
        const_made = sem("const_made")
        mask_cast = sem("mask_cast")
        mask_T = sem("mask_T")
        mask_taken = sem("mask_taken")
        adj_loaded = sem("adj_loaded")
        adj_free = sem("adj_free")
        x_loaded = sem("x_loaded")
        x_free = sem("x_free")
        out_stored = [sem(f"out_stored{n}") for n in range(2)]
        adjT_ps = sem("adjT_ps")
        adjT_sb = sem("adjT_sb")
        nb_ready = sem("nb_ready")
        counts_ps = sem("counts_ps")
        counts_taken = sem("counts_taken")
        cum_ps = sem("cum_ps")
        gone_ready = sem("gone_ready")
        rank_ps = sem("rank_ps")
        goneT_ps = sem("goneT_ps")
        val_ready = sem("val_ready")
        sortmask_ps = sem("sortmask_ps")
        sortmask_sb = sem("sortmask_sb")
        cum1_ps = sem("cum1_ps")
        slot1_ready = sem("slot1_ready")
        cum2_ps = sem("cum2_ps")
        slot2_ready = sem("slot2_ready")
        deg_ps = sem("deg_ps")
        over_ready = sem("over_ready")
        over_ps = sem("over_ps")
        long_ready = sem("long_ready")
        varA = sem("varA")
        stdA = sem("stdA")
        varB = sem("varB")
        stdB = sem("stdB")
        h0_ready = sem("h0_ready")
        feat0_ps = sem("feat0_ps")
        feat0_sb = sem("feat0_sb")
        pre0_ps = sem("pre0_ps")
        tanh_sb = sem("tanh_sb")
        dh0_ps = sem("dh0_ps")
        parts1_ready = sem("parts1_ready")
        pick1_ready = sem("pick1_ready")
        fetched1_ps = sem("fetched1_ps")
        fetched1_sb = sem("fetched1_sb")
        sorted_ops = [sem(f"sorted_ops{n}") for n in range(2)]
        agg_ready = sem("agg_ready")
        aggT_ps = sem("aggT_ps")
        aggT_sb = sem("aggT_sb")
        hid_ps = sem("hid_ps")
        hid_sb = sem("hid_sb")
        y1_ps = sem("y1_ps")
        x2_ready = sem("x2_ready")
        h2_ready = sem("h2_ready")
        permT_saved = sem("permT_saved")
        h2T_ps = sem("h2T_ps")
        h2T_sb = sem("h2T_sb")
        v_ps = sem("v_ps")
        v_sb = sem("v_sb")
        u_ps = sem("u_ps")
        u_sb = sem("u_sb")
        parts2_ready = sem("parts2_ready")
        up_ready = sem("up_ready")
        pick2_ready = sem("pick2_ready")
        fetched2_ps = sem("fetched2_ps")
        taken2 = sem("taken2")
        summed2 = sem("summed2")
        acc2_ready = sem("acc2_ready")
        acc2T_ps = sem("acc2T_ps")
        acc2T_sb = sem("acc2T_sb")
        ysort_ps = sem("ysort_ps")
        ysort_sb = sem("ysort_sb")
        yp_ready = sem("yp_ready")
        y2_ps = sem("y2_ps")
        small_ready = sem("small_ready")
        small_done = sem("small_done")
        tok_ready = sem("tok_ready")
        cT_ps = sem("cT_ps")
        cT_sb = sem("cT_sb")
        cb_ps = sem("cb_ps")
        cb_sb = sem("cb_sb")
        LR_ps = sem("LR_ps")
        LR_sb = sem("LR_sb")
        pair_ps = sem("pair_ps")
        clamped = sem("clamped")
        hz_sb = sem("hz_sb")
        logs_sb = sem("logs_sb")
        qp_ready = sem("qp_ready")
        exps_sb = sem("exps_sb")
        s_clipped = sem("s_clipped")
        log1_sb = sem("log1_sb")
        diff_ready = sem("diff_ready")
        z_ready = sem("z_ready")
        sig_sb = sem("sig_sb")
        att_ready = sem("att_ready")
        weight_ready = sem("weight_ready")
        feat3_ready = sem("feat3_ready")
        support_ps = sem("support_ps")
        support_sb = sem("support_sb")
        out_ready = sem("out_ready")
        valid_ps = sem("valid_ps")
        valid_used = sem("valid_used")
        row_ps = sem("row_ps")
        row_used = sem("row_used")
        MORE = W * sum(N - k for k in K2Q)
        more_picked = sem("more_picked")
        more_ps = sem("more_ps")
        more_summed = sem("more_summed")

        NCONST = 16
        MADE = 22
        SMALL = 5
        NU = len(UNITS)
        (X2, WL, WS, BM, LAM, LB, LW, NLW, CC, DD, DF, SN, S0, S1, S2, S3, S4, S5, NORM, DK, M1, MC,
         ST0, ST1, ST2, ST3) = range(26)
        ANYC, NBC, KEYC, RANK1, RANK2, ONC, A0, A1, A2, AM, AMC = range(4, 15)

        SORT_LAG = 2
        SORT_OPS = 6
        sorts = []
        for k in range(K1):
            steps = []
            for n, c in enumerate(CLASSES):
                c["last"] = [max(b for _, b, _, _ in step) for step in c["steps"]]
                c["last"] = [max(c["last"][:m + 1]) for m in range(len(c["steps"]))]
                steps += [(n, m) for m in range(len(c["steps"])) if c["last"][m] == k]
            size = SORT_OPS
            for n, m in steps:
                if size >= SORT_OPS:
                    sorts.append((k, []))
                    size = 0
                sorts[-1][1].append((n, m))
                size += sum(hi + lo for _, _, hi, lo in CLASSES[n]["steps"][m])
        A_PARTS = (["masks", "masksT", "keys", "gone", "ranks", "count", "slot1", "slot2", "lengths", "long"] +
                   [("layer0", i) for i in range(G + 2)] + ["x1", "h1"] +
                   [x for k in range(K1 + SORT_LAG)
                    for x in ([("slot", k)] if k < K1 else []) +
                    [("sort", i) for i, (last, _) in enumerate(sorts) if last == k - SORT_LAG]] +
                   [("quantile", i) for i in range(len(CLASSES))] + ["agg"] +
                   [("mlp", i) for i in range(G + 2)] + ["x2"])
        B_PARTS = (["layernorm2", "h2"] + [("uv", i) for i in range(7)] + ["uv_parts"] +
                   [("unit", i) for i in range(NU)] +
                   ["sum2", "y_sorted", "y2", "layernorm3", "h3", "values", "tokens", "columns"] +
                   [("pair", i, j) for i in range(G + 2) for j in range(3)] +
                   [("logit", i) for i in range(G + 2)] +
                   ["weights", "support", "step", "tanh", "moved", "norm"])

        STREAMS = (
            "ABABBBABBABBBABBABABABAABABABABABABABABBABABAAAAAAAAAABAAABAABABBABAABAAAABABABBBABAABBBAB"
            "BAABABAAABABABAABBAABAAAAABAABABAAABAABAAABAAABABAAABAABBBBAABBBBBBBBABBABABBABABBAA")
        assert STREAMS.count("A") == len(A_PARTS) and STREAMS.count("B") == len(B_PARTS)
        ORDER = [(s, (A_PARTS if s == "A" else B_PARTS)[STREAMS[:n].count(s)]) for n, s in enumerate(STREAMS)]

        def run(engine, A, B_):
            def both(g, parity, turn, g_next, turn_next):
                streams = {"B": B_(g, parity, turn), "A": A(g_next, 1 - parity, turn_next)}
                at = {s: next(streams[s], None) for s in streams}
                for s, part in ORDER:
                    if at[s] == part:
                        at[s] = next(streams[s], None)
                assert at == {"A": None, "B": None}, at

            def alone(parts):
                for _ in parts:
                    pass

            alone(A(0, 0, 0))
            with engine.Fori(0, NG // 2 - 1) as m:
                g = m * 2
                both(g, 0, m, g + 1, m)
                both(g + 1, 1, m, g + 2, m + 1)
            both(NG - 2, 0, NG // 2 - 1, NG - 1, NG // 2 - 1)
            alone(B_(NG - 1, 1, NG // 2 - 1))

        def is_first(g):
            return isinstance(g, int) and g == 0

        block = ctx.enter_context(nc.Block())

        @block.sync
        def _(sync):
            def const(dst, src):
                sync.dma_start(dst, src).then_inc(const_loaded, 16)
            x_v = x.rearrange("(g b) (t p) c -> p g (b t) c", g=NG, p=P)
            adj_v = adj.rearrange("(g b) (t p) j -> p g (b t) j", g=NG, p=P)

            def load(g):
                sync.dma_start(x_in[:, :, :], x_v[:, bass.ds(g, 1)].rearrange("p o t c -> p (o t) c")
                               ).then_inc(x_loaded, 16)
                sync.dma_start(adj_in[:, :, :], adj_v[:, bass.ds(g, 1)].rearrange("p o t j -> p (o t) j")
                               ).then_inc(adj_loaded, 16)
            load(0)
            const(w1_0[:, :, :], W1_0.rearrange("(a c) o -> c a o", a=2))
            const(w2_0[:, :], W2_0)
            const(w1_1[:, :], W1_1)
            const(w2_1[:, :], W2_1)
            const(w1_2[:, :, :], W1_2.rearrange("(a c) o -> c a o", a=2))
            const(w2_2[:, :, :], W2_2.rearrange("(a c) o -> c a o", a=2))
            const(bias0[:, :], b1_0.rearrange("(c o) -> c o", o=1))
            const(bias1[:, :], b1_1.rearrange("(c o) -> c o", o=1))
            const(brow[:, 0, :], b2_0.rearrange("(o c) -> o c", o=1))
            const(brow[:, 1, :], b2_1.rearrange("(o c) -> o c", o=1))
            const(b2_all[:, :], b2_2.rearrange("(o c) -> o c", o=1).broadcast_to([P, F]))
            const(brow2[:, :], b1_2.rearrange("(o c) -> o c", o=1))
            const(att_w[:, 0, :], att_W[0:F, :].rearrange("c o -> o c").broadcast_to([P, F]))
            const(att_w[:, 1, :], att_W[F:2 * F, :].rearrange("c o -> o c").broadcast_to([P, F]))
            const(att_c[:, :], att_b.rearrange("(o c) -> o c", o=1).broadcast_to([P, 1]))
            const(mask_in[:, :], nodemask.rearrange("b (t p) -> (b t) p", p=P))
            with sync.Fori(1, NG) as g:
                sync.wait_ge(adjT_ps, g * G)
                sync.wait_ge(x_free, g)
                sync.wait_ge(adj_free, g)
                sync.nop(nofuse=True)
                load(g)

        @block.gpsimd
        def _(pool):
            g_ = nc.gpsimd
            made = [0]

            def make(ins):
                made[0] += 1
                ins.then_inc(const_made, 1)

            make(g_.memset(identf[:, :], 0.0))
            make(g_.memset(identb[:, :], 0.0))
            make(g_.memset(tri[:, :], 1.0))
            make(g_.memset(onesb[:, :], 1.0))
            make(g_.memset(onesf[:, :], 1.0))
            make(g_.memset(eye[:, :, :], 0.0))
            make(g_.memset(noteye[:, :, :], 1.0))
            pool.wait_ge(const_made, 7)
            for m in (identf, identb):
                make(g_.affine_select(out=m[:, :], in_=m[:, :], compare_op=ALU.not_equal, fill=1.0, base=0,
                                      pattern=[[-1, P]], channel_multiplier=1))
            make(g_.affine_select(out=tri[:, :], in_=tri[:, :], compare_op=ALU.is_ge, fill=0.0, base=0,
                                  pattern=[[1, P]], channel_multiplier=-1))
            for m, v in ((eye, 1.0), (noteye, 0.0)):
                make(g_.affine_select(out=m[:, :, :], in_=m[:, :, :], compare_op=ALU.not_equal, fill=v, base=0,
                                      pattern=[[P, HALVES], [-1, N]], channel_multiplier=1))
            make(g_.iota(count_i[:, :], pattern=[[1, N]], base=0, channel_multiplier=0))
            make(g_.iota(part_i[:, :], pattern=[[0, G], [P, HALVES]], base=0, channel_multiplier=1))
            for s in range(2):
                pool.wait_ge(const_made, made[0])
                make(g_.iota(rank_i[s * R:(s + 1) * R, :], pattern=[[R, Q], [0, W]], base=0, channel_multiplier=1))
            pool.wait_ge(const_made, made[0])
            for n, c in enumerate(CLASSES):
                make(g_.memset(caps[:, 0, c["tiles"][0]:c["tiles"][1]], float(c["k"])))
            for q in range(Q):
                make(g_.memset(caps[:, 1, q * W:(q + 1) * W], float(K2Q[q])))
            assert made[0] == MADE

            def A(g, parity, turn):
                return iter(())

            def B_(g, parity, turn):
                for i in range(G + 2):
                    if 1 <= i <= G:
                        j = i - 1
                        yield "pair", i, 1
                        pool.wait_ge(logs_sb, g * G + (j + 1))
                        g_.tensor_tensor(bq[:, j], bn[:, j], bd[:, j], ALU.subtract).then_inc(qp_ready, 1)
                        pool.wait_ge(qp_ready, g * (2 * G) + (2 * j + 1))
                        g_.tensor_tensor(bn[:, j], bn[:, j], bd[:, j], ALU.add).then_inc(qp_ready, 1)
                    if i >= 2:
                        j = i - 2
                        yield "pair", i, 2
                        pool.wait_ge(log1_sb, g * G + (j + 1))
                        g_.tensor_tensor(bd[:, j], bd[:, j], bb[:, j % 2], ALU.subtract).then_inc(diff_ready, 1)
                for i in range(G):
                    yield "logit", i + 2
                    pool.wait_ge(sig_sb, g * G + (i + 1))
                    g_.tensor_tensor(bz[:, i], bz[:, i], adjT[parity][:, i], ALU.mult).then_inc(att_ready, 1)

            run(pool, A, B_)

        @block.scalar
        def _(act):
            s_ = nc.scalar

            act.wait_ge(const_loaded, 16 * NCONST)
            act.wait_ge(mask_T, 1)
            s_.copy(mask_col[:, :, :], ps[:, 0, 0:B * HALVES].rearrange("p (g t) -> p g t", g=NG)
                    ).then_inc(mask_taken, 1)

            def A(g, parity, turn):
                def std(n):
                    act.wait_ge(varA, g * 2 + (n + 1))
                    s_.activation(smA[:, 2, :], smA[:, 1, :], ACT.Sqrt).then_inc(stdA, 1)

                yield "masks"
                for b in range(G):
                    act.wait_ge(adjT_ps, g * G + (b + 1))
                    s_.copy(adjT[parity][:, b], ps[:, b, :].rearrange("p (a n) -> p a n", a=HALVES)
                            ).then_inc(adjT_sb, 1)
                std(0)
                yield "ranks"
                for m, dst in enumerate((val_s, any_s)):
                    for b in range(G):
                        act.wait_ge(sortmask_ps, g * (2 * G) + (m * G + b + 1))
                        s_.copy(dst[:, b], ps[:, b, :].rearrange("p (a n) -> p a n", a=HALVES)
                                ).then_inc(sortmask_sb, 1)
                for i in range(G + 1):
                    yield "layer0", i
                    if i < G:
                        act.wait_ge(feat0_ps, g * G + (i + 1))
                        s_.copy(feat[:, i % 2], ps[0:F, i % 2, :].rearrange("p (a n) -> p a n", a=2)
                                ).then_inc(feat0_sb, 1)
                    if i >= 1:
                        r = (i - 1) % 2
                        act.wait_ge(pre0_ps, g * G + i)
                        s_.activation(tanh_t[:, r, :], ps[0:F, 2, r * N:(r + 1) * N], ACT.Tanh, bias=bias0[:, :]
                                      ).then_inc(tanh_sb, 1)
                yield "x1"
                std(1)
                for k in range(K1):
                    yield "slot", k
                    act.wait_ge(fetched1_ps, g * K1 + (k + 1))
                    classes = [c for c in CLASSES if k < c["k"]]
                    for c in classes:
                        last = s_.copy(c["buf"][:, k, :], ps[:, k % 4, c["tiles"][0] * F:c["tiles"][1] * F])
                    last.then_inc(fetched1_sb, 1)
                for i in range(G + 1):
                    yield "mlp", i
                    if i < G:
                        act.wait_ge(aggT_ps, g * G + (i + 1))
                        s_.copy(feat[:, i % 2, 0, :], ps[0:F, i % 2, 0:N]).then_inc(aggT_sb, 1)
                    if i >= 1:
                        r = (i - 1) % 2
                        act.wait_ge(hid_ps, g * G + i)
                        s_.activation(hid[:, r, :], ps[:, 2, r * N:(r + 1) * N], ACT.Relu, bias=bias1[:, :]
                                      ).then_inc(hid_sb, 1)

            def B_(g, parity, turn):
                def std(n):
                    act.wait_ge(varB, g * 2 + (n + 1))
                    s_.activation(smB[:, ST2, :], smB[:, ST1, :], ACT.Sqrt).then_inc(stdB, 1)

                yield "layernorm2"
                act.wait_ge(x2_ready, g + 1)
                s_.copy(permT2, permT[:, :, :, :]).then_inc(permT_saved, 1)
                std(0)
                for i in range(7):
                    yield "uv", i
                    if i in (1, 2, 4, 5):
                        b = (None, 0, 1, None, 2, 3)[i]
                        act.wait_ge(v_ps, g * G + (b + 1))
                        minus_v = ps[:, 6 + b % 2, 0:2 * H2].rearrange("p (t c) -> p t c", t=2)
                        s_.copy(v2[:, 2 * b:2 * b + 2, :], minus_v)
                        s_.copy(vp[:, 2 * b:2 * b + 2, 0, :], minus_v).then_inc(v_sb, 1)
                    if i in (0, 1, 3, 4):
                        b = (0, 1, None, 2, 3)[i]
                        r = b % 2
                        act.wait_ge(h2T_ps, g * G + (b + 1))
                        s_.copy(featB[:, r, 0, :], ps[0:F, 4, r * N:(r + 1) * N])
                        s_.copy(featB[:, r, 1, :], ps[0:F, 5, r * N:(r + 1) * N]).then_inc(h2T_sb, 1)
                    if i in (2, 6):
                        w = i // 4
                        act.wait_ge(u_ps, g * W + (w + 1))
                        for dst in (u2, up[0]):
                            last = s_.copy(dst.rearrange("p (q w) c -> p q w c", w=W)[:, :, w, :].rearrange(
                                "p (a e) c -> p a e c", e=2), ps[:, 4:8, :][:, 2 * w:2 * w + 2, 0:2 * H2].rearrange(
                                    "p a (e c) -> p a e c", e=2))
                        last.then_inc(u_sb, 1)
                yield "sum2"
                for w in range(W):
                    act.wait_ge(acc2T_ps, g * W + (w + 1))
                    s_.copy(acc2T[:, w, :].rearrange("p (a n) -> p a n", a=2), ps[0:H2 // 2, 4 + 2 * w:6 + 2 * w, :]
                            ).then_inc(acc2T_sb, 1)
                yield "y_sorted"
                act.wait_ge(ysort_ps, g + 1)
                s_.copy(y_sorted.rearrange("p u c -> p (u c)"), ps[:, 4, :])
                s_.copy(yp[:, 0, :], ps[:, 4, :]).then_inc(ysort_sb, 1)
                yield "layernorm3"
                std(1)
                yield "h3"
                act.wait_ge(small_ready, g * SMALL + 1)
                s_.activation(smB[:, NORM, :], smB[:, X2, :], ACT.Sqrt).then_inc(small_done, 1)
                yield "values"
                act.wait_ge(small_ready, g * SMALL + 2)
                s_.activation(smB[:, S0, :], smB[:, S2, :], ACT.Ln, bias=1.0)
                s_.activation(smB[:, S1, :], smB[:, S2, :], ACT.Ln, scale=-1.0, bias=1.0).then_inc(small_done, 1)
                yield "tokens"
                act.wait_ge(cT_ps, g + 1)
                s_.copy(cT[:, :], ps[0:T, 4, 0:P]).then_inc(cT_sb, 1)
                yield "columns"
                act.wait_ge(cb_ps, g + 1)
                s_.copy(cb[:, :, :], ps[:, 5:7, :].rearrange("p a (b n) -> p (a b) n", n=N)).then_inc(cb_sb, 1)
                for i in range(G + 2):
                    yield "pair", i, 0
                    if i < G:
                        act.wait_ge(LR_ps, g * (2 * G) + (2 * i + 1))
                        s_.copy(LR[:, 0:2, :], ps[0:FX, 7, :].rearrange("p (b n) -> p b n", n=N)).then_inc(LR_sb, 1)
                    if i >= 2:
                        j = i - 2
                        act.wait_ge(s_clipped, g * G + (j + 1))
                        if j >= 2:
                            act.wait_ge(diff_ready, g * G + (j - 1))
                        s_.activation(bd[:, j], bq[:, j], ACT.Ln, bias=1.0)
                        s_.activation(bb[:, j % 2], bq[:, j], ACT.Ln, scale=-1.0, bias=1.0).then_inc(log1_sb, 1)
                    if 1 <= i <= G:
                        j = i - 1
                        act.wait_ge(clamped, g * G + (j + 1))
                        s_.activation(bn[:, j], bn[:, j], ACT.Ln)
                        s_.activation(bd[:, j], bd[:, j], ACT.Ln).then_inc(logs_sb, 1)
                    yield "pair", i, 1
                    if i < G:
                        act.wait_ge(LR_ps, g * (2 * G) + (2 * i + 2))
                        s_.copy(LR[:, 2:4, :], ps[0:FX, 7, :].rearrange("p (b n) -> p b n", n=N)).then_inc(LR_sb, 1)
                    yield "pair", i, 2
                    if i < G:
                        act.wait_ge(pair_ps, g * G + (i + 1))
                        s_.copy(bz[:, i], ps[:, 6, :].rearrange("p (a n) -> p a n", a=HALVES)).then_inc(hz_sb, 1)
                    if 1 <= i <= G:
                        j = i - 1
                        act.wait_ge(qp_ready, g * (2 * G) + (2 * j + 2))
                        s_.activation(bq[:, j], bq[:, j], ACT.Exp, scale=0.5)
                        s_.activation(bn[:, j], bn[:, j], ACT.Exp, scale=-0.5).then_inc(exps_sb, 1)
                for i in range(G):
                    yield "logit", i + 2
                    act.wait_ge(z_ready, g * G + (i + 1))
                    s_.activation(bz[:, i], bz[:, i], ACT.Sigmoid).then_inc(sig_sb, 1)
                yield "weights"
                act.wait_ge(support_ps, g + 1)
                s_.copy(sp[:, :, :].rearrange("p (a b) c -> p a b c", a=2),
                        ps[:, 4:6, :].rearrange("p a (b c) -> p a b c", b=4)[:, :, :, 0:F + 1]
                        ).then_inc(support_sb, 1)
                for n, (part, dst, src, func) in enumerate((("support", S1, S0, ACT.Sqrt), ("step", S3, S2, ACT.Tanh),
                                                            ("tanh", S1, S0, ACT.Sqrt))):
                    yield part
                    act.wait_ge(small_ready, g * SMALL + (3 + n))
                    s_.activation(smB[:, dst, :], smB[:, src, :], func).then_inc(small_done, 1)
                yield "moved"
                act.wait_ge(out_ready, g + 1)
                act.dma_start(out.rearrange("(g b) (t p) c -> p g (b t) c", g=NG, p=P)[:, bass.ds(g, 1)]
                              .rearrange("p o t c -> p (o t) c"), xs[parity][:, :, :]).then_inc(out_stored[parity], 16)

            run(act, A, B_)
            for s in out_stored:
                act.wait_ge(s, 16 * (NG // 2))

        @block.vector
        def _(dve):
            v_ = nc.vector
            settle = v_.drain

            def over_tiles(row, width=F):
                return row.unsqueeze(2).broadcast_to([P, T, width])

            def flat(t):
                return t.rearrange("p a b n -> p (a b n)")

            def f2(t):
                return t.rearrange("p a n -> p (a n)")

            def bank_pairs(bank):
                return ps[:, bank, :].rearrange("p (a n) -> p a n", a=HALVES)

            def by_tile(t):
                return t.rearrange("p g a n -> p (g a) n")

            banksA = ps[:, 0:4, :].rearrange("p g (a n) -> p g a n", a=HALVES)

            def layernorm_variance(src, xc, sq, stat, rows, var_sem):
                r0, r1, _, _ = rows
                v_.reduce_sum(stat[:, r0, :], src, AX.X)
                settle()
                v_.tensor_scalar(stat[:, r0, :], stat[:, r0, :], -1.0 / F, None, ALU.mult)
                settle()
                v_.tensor_tensor(xc[:, :, :], src, over_tiles(stat[:, r0, :]), ALU.add)
                settle()
                v_.tensor_tensor(sq[:, :, :], xc[:, :, :], xc[:, :, :], ALU.mult)
                settle()
                v_.reduce_sum(stat[:, r1, :], sq[:, :, :], AX.X)
                settle()
                v_.tensor_scalar(stat[:, r1, :], stat[:, r1, :], 1.0 / F, EPS, ALU.mult, ALU.add).then_inc(var_sem, 1)

            def layernorm_relu(dst, xc, stat, rows, std_sem, n, g):
                _, _, r2, r3 = rows
                dve.wait_ge(std_sem, g * 2 + (n + 1))
                v_.reciprocal(stat[:, r3, :], stat[:, r2, :])
                settle()
                v_.tensor_tensor(dst[:, :, :], xc[:, :, :], over_tiles(stat[:, r3, :]), ALU.mult)
                settle()
                return v_.tensor_scalar(dst[:, :, :], dst[:, :, :], 0.0, None, ALU.max)

            def split_in_three(value, parts, rest):
                v_.tensor_copy(parts[0], value)
                settle()
                return split_rest(value, parts, rest)

            def split_rest(value, parts, rest):
                v_.tensor_tensor(rest, value, parts[0], ALU.subtract)
                settle()
                v_.tensor_copy(parts[1], rest)
                settle()
                return v_.tensor_tensor(parts[2], rest, parts[1], ALU.subtract)

            def general_quantiles(g):
                v_.tensor_copy(over[:, 0:1], over[:, 0:1]).then_inc(row_used, 1)
                with dve.Fori(0, T) as t:
                    dve.wait_ge(valid_ps, g * T + t + 1)
                    v_.tensor_scalar(all_valid, psb[:, 1, 0:N], 0.5, None, ALU.is_gt).then_inc(valid_used, 1)
                    settle()
                    v_.reduce_sum(over[:, 2:3], all_valid, AX.X)
                    settle()
                    for n, (tau, weight) in enumerate(TAUS):
                        v_.tensor_scalar(over[:, 3:4], over[:, 2:3], -1.0, -(1.0 - tau), ALU.add, ALU.mult)
                        settle()
                        v_.tensor_scalar(all_wt, count_row[:, :], over[:, 3:4], None, ALU.add)
                        settle()
                        v_.scalar_tensor_tensor(all_wt, all_wt, -1.0, all_wt, ALU.mult, ALU.max)
                        settle()
                        v_.tensor_scalar(all_wt, all_wt, -1.0, 1.0, ALU.mult, ALU.add)
                        settle()
                        v_.tensor_scalar(all_wt if n else all_w, all_wt, 0.0, weight, ALU.max, ALU.mult)
                        settle()
                        if n:
                            v_.tensor_tensor(all_w, all_w, all_wt, ALU.add)
                            settle()
                    with dve.Fori(0, F) as c:
                        dve.wait_ge(row_ps, g * (T * F) + t * F + c + 1)
                        v_.tensor_tensor(all_left, ps[:, 2, 0:N], all_valid, ALU.mult).then_inc(row_used, 1)
                        settle()
                        for r in range(0, N, 8):
                            v_.max(all_sorted[:, r:r + 8], all_left)
                            settle()
                            v_.match_replace(all_left, all_sorted[:, r:r + 8], all_left, -1.0)
                            settle()
                        v_.tensor_tensor(all_prod, all_sorted, all_w, ALU.mult)
                        settle()
                        v_.reduce_sum(all_agg[:, bass.ds(t, 1), bass.ds(c, 1)].rearrange("p a b -> p (a b)"), all_prod,
                                      AX.X)
                        settle()
                for s in range(2):
                    for e in range(2):
                        for a in range(HALVES):
                            v_.tensor_copy(agg[s * R:(s + 1) * R, (2 * a + e) * W:(2 * a + e + 1) * W, :],
                                           all_agg.rearrange("p (w s a) c -> p w s a c", s=2, a=HALVES)[
                                               e * R:(e + 1) * R, :, s, a, :])
                            settle()

            def general_relu_sum(g, parity):
                settle()
                for q, k2 in enumerate(K2Q):
                    for w in range(W):
                        u = q * W + w
                        v_.tensor_scalar(more_h, u2[:, u, :], 0.0, -float(N - k2), ALU.max, ALU.mult)
                        settle()
                        v_.tensor_tensor(acc2[:, u, :], acc2[:, u, :], more_h, ALU.add)
                        settle()
                at = 0
                for q, k2 in enumerate(K2Q):
                    for w in range(W):
                        u = q * W + w
                        v_.memset(overB[:, :], float(k2 + 1))
                        settle()
                        with dve.Fori(0, N - k2) as k:
                            v_.tensor_scalar(pick2[:, 0, 0:4, 0:R], by_tile(slot2[parity][:, :, :, :])[
                                :, 4 * w:4 * w + 4, q * R:(q + 1) * R], overB[:, :], None, ALU.is_equal
                            ).then_inc(more_picked, 1)
                            dve.wait_ge(more_ps, g * MORE + k + (at + 1))
                            v_.tensor_tensor(more_h, u2[:, u, :], ps[:, 4, 0:H2], ALU.add)
                            v_.tensor_scalar(overB[:, :], overB[:, :], 1.0, None, ALU.add)
                            settle()
                            v_.scalar_tensor_tensor(acc2[:, u, :], more_h, 0.0, acc2[:, u, :],
                                                    ALU.max, ALU.add).then_inc(more_summed, 1)
                            settle()
                        at += N - k2

            dve.wait_ge(const_loaded, 16 * NCONST)
            v_.tensor_copy(mask_f[:, :], mask_in[:, :]).then_inc(mask_cast, 1)
            v_.tensor_tensor(wsum_2[:, :], w1_2[:, 0, :], w1_2[:, 1, :], ALU.add)
            settle()
            v_.tensor_scalar(w1_2[:, 1, :], w1_2[:, 1, :], -1.0, None, ALU.mult).then_inc(mask_cast, 1)
            dve.wait_ge(const_made, MADE)
            v_.tensor_copy(count_row[:, :], count_i[:, :])
            v_.memset(overB[:, :], 0.0)
            v_.tensor_copy(node_col[:, :], part_i[:, :])
            v_.tensor_copy(rank_col[:, :], rank_i[:, :])
            dve.wait_ge(mask_taken, 1)
            settle()

            def A(g, parity, turn):
                def row(i):
                    return smA[:, i, :]

                yield "masks"
                dve.wait_ge(adj_loaded, g * 16 + 16)
                v_.tensor_scalar(by_tile(any_m), adj_in[:, :, :], 0.0, None, ALU.is_gt).then_inc(adj_free, 1)
                settle()
                v_.tensor_tensor(nb_m.rearrange("p g a n -> p g (a n)"), any_m.rearrange("p g a n -> p g (a n)"),
                                 noteye[:, :, :].rearrange("p a n -> p (a n)").unsqueeze(1).broadcast_to([P, G, 512]),
                                 ALU.mult)
                dve.wait_ge(x_loaded, g * 16 + 16)
                layernorm_variance(x_in[:, :, :], xcA, sqA, smA, (0, 1, 2, 3), varA)
                yield "masksT"
                layernorm_relu(hA, xcA, smA, (0, 1, 2, 3), stdA, 0, g).then_inc(h0_ready, 1)
                dve.wait_ge(adjT_sb, g * G + G)
                v_.tensor_scalar(any_T, adjT[parity][:, :, :, :], 0.0, None, ALU.is_gt)
                settle()
                v_.tensor_tensor(nb_T.rearrange("p g a n -> p g (a n)"), any_T.rearrange("p g a n -> p g (a n)"),
                                 noteye[:, :, :].rearrange("p a n -> p (a n)").unsqueeze(1).broadcast_to([P, G, 512]),
                                 ALU.mult).then_inc(nb_ready, 1)
                yield "keys"

                dve.wait_ge(counts_ps, g + 1)
                v_.tensor_copy(row(NBC), ps[:, 0, 0:T])
                v_.tensor_copy(row(ANYC), ps[:, 0, T:2 * T])
                v_.tensor_scalar(key_row.rearrange("p (a b) n -> p a (b n)", a=2), ps[:, 1:3, :], float(N), None,
                                 ALU.mult).then_inc(counts_taken, 1)
                settle()
                v_.tensor_tensor(key_row, key_row, count_row[:, :].unsqueeze(1).broadcast_to([P, G, N]), ALU.add)
                v_.scalar_tensor_tensor(row(KEYC), row(ANYC), float(N), node_col[:, :], ALU.mult, ALU.add)
                v_.tensor_copy(deg_node[parity][:, :], row(ANYC))
                v_.tensor_copy(row(AMC), mask_col[:, bass.ds(g, 1), :].rearrange("p o t -> p (o t)"))
                v_.tensor_scalar(row(RANK1), row(NBC), 0.5, 0.25, ALU.mult, ALU.add)
                settle()
                v_.scalar_tensor_tensor(row(ONC), row(NBC), DILATE_OVER, row(AMC), ALU.is_gt, ALU.mult)
                v_.tensor_scalar(row(RANK1), row(RANK1), ROUND, None, ALU.add)
                settle()
                v_.tensor_scalar(row(RANK1), row(RANK1), ROUND, None, ALU.subtract)
                settle()
                v_.scalar_tensor_tensor(row(RANK1), row(RANK1), FAR, row(ONC), ALU.subtract, ALU.mult)
                settle()
                v_.tensor_scalar(row(RANK2), row(RANK1), 2.0, 2 * FAR, ALU.mult, ALU.add)
                settle()
                v_.tensor_scalar(row(RANK1), row(RANK1), FAR, None, ALU.add)
                v_.tensor_tensor(less, key_row.unsqueeze(2).broadcast_to(PAIR),
                                 row(KEYC).rearrange("p (g a) -> p g a", a=HALVES).unsqueeze(3).broadcast_to(PAIR),
                                 ALU.is_gt)
                settle()
                yield "gone"
                dve.wait_ge(cum_ps, g + 1)
                v_.tensor_tensor(by_tile(at1), by_tile(banksA), over_tiles(row(RANK1), N), ALU.is_equal)
                v_.tensor_tensor(by_tile(at2), by_tile(banksA), over_tiles(row(RANK2), N), ALU.is_equal)
                settle()
                v_.tensor_tensor(at1, at1, at2, ALU.add)
                settle()
                v_.tensor_tensor(gone, at1, nb_m, ALU.mult).then_inc(gone_ready, 1)
                yield "ranks"

                dve.wait_ge(rank_ps, g + 1)
                v_.tensor_copy(row(A0), ps[:, 0, 0:T])
                settle()
                if not is_first(g):
                    dve.wait_ge(h2T_ps, g * G)
                    dve.wait_ge(permT_saved, g)
                v_.tensor_tensor(by_tile(perm[:, :, :, :]), count_row[:, :].unsqueeze(1).broadcast_to([P, T, N]),
                                 over_tiles(row(A0), N), ALU.is_equal)
                for q in range(Q):
                    v_.tensor_scalar(permT[:, q], ps[:, 1, :].rearrange("p (w n) -> p w n", w=W),
                                     rank_col[:, q * W:q * W + 1], None, ALU.is_equal)
                dve.wait_ge(goneT_ps, g + 1)
                v_.tensor_tensor(at1.rearrange("p (a b) h n -> p a (b h n)", a=2),
                                 gone.rearrange("p (a b) h n -> p a (b h n)", a=2), psb[:, 2:4, :], ALU.add)
                settle()
                v_.scalar_tensor_tensor(flat(val_m), flat(at1), 0.5, flat(nb_m), ALU.is_lt, ALU.mult)
                settle()
                v_.tensor_tensor(val_m.rearrange("p g a n -> p g (a n)"), val_m.rearrange("p g a n -> p g (a n)"),
                                 eye[:, :, :].rearrange("p a n -> p (a n)").unsqueeze(1).broadcast_to([P, G, 512]),
                                 ALU.add).then_inc(val_ready, 1)
                yield "slot1"
                dve.wait_ge(cum1_ps, g + 1)
                v_.tensor_tensor(slot1[:, :, :, :], banksA, val_s, ALU.mult).then_inc(slot1_ready, 1)
                yield "slot2"
                dve.wait_ge(cum2_ps, g + 1)
                v_.tensor_tensor(slot2[parity][:, :, :, :], banksA, any_s, ALU.mult).then_inc(slot2_ready, 1)
                yield "lengths"
                dve.wait_ge(deg_ps, g + 1)
                v_.tensor_copy(deg_sorted[parity][:, :, :], ps[:, 0, 0:2 * U].rearrange("p (a t) -> p a t", a=2))
                settle()
                v_.tensor_tensor(row(A0), deg_sorted[parity][:, 0, :], caps[:, 0, :], ALU.subtract)
                v_.tensor_tensor(row(A1), deg_sorted[parity][:, 1, :], caps[:, 1, :], ALU.subtract)
                settle()
                v_.tensor_tensor(row(A0), row(A0), row(A1), ALU.max)
                settle()
                v_.reduce_max(over[:, 0:1], row(A0), AX.X).then_inc(over_ready, 1)
                yield "long"
                dve.wait_ge(over_ps, g + 1)
                v_.reduce_max(over[0:1, 1:2], ps[0:1, 1, 0:P], AX.X)
                settle()
                v_.tensor_scalar(is_long[parity][:, :], over[0:1, 1:2], 0.0, None, ALU.is_gt).then_inc(long_ready, 1)

                yield "x1"
                dve.wait_ge(dh0_ps, g * G + G)
                if isinstance(turn, int) and turn == 0:
                    pass
                else:
                    dve.wait_ge(out_stored[parity], turn * 16)
                v_.tensor_tensor(xs[parity][:, :, :], x_in[:, :, :], ps[:, 3, :].rearrange("p (t c) -> p t c", c=F),
                                 ALU.add).then_inc(x_free, 1)
                settle()
                layernorm_variance(xs[parity][:, :, :], xcA, sqA, smA, (0, 1, 2, 3), varA)
                yield "h1"
                layernorm_relu(hA, xcA, smA, (0, 1, 2, 3), stdA, 1, g)
                settle()
                split_in_three(hA[:, :, :], [hpA[:, :, i, :] for i in range(3)], xcA[:, :, :]).then_inc(parts1_ready, 1)

                bufs = [list(range(c["k"])) for c in CLASSES]
                spares = [list(range(c["k"], c["k"] + SPARE)) for c in CLASSES]
                done = [0, 0]

                def sort_step(n, m):
                    c, buf, spare = CLASSES[n], bufs[n], spares[n]
                    base = g * c["ops"]
                    if done[n]:
                        dve.wait_ge(sorted_ops[n], base + done[n])
                    tops = {}
                    for a, b, hi, lo in c["steps"][m]:
                        if hi:
                            tops[a] = (spare.pop(0), done[n] + 1)
                            v_.tensor_tensor(c["buf"][:, tops[a][0], :], c["buf"][:, buf[a], :], c["buf"][:, buf[b], :],
                                             ALU.max).then_inc(sorted_ops[n], 1)
                            done[n] += 1
                    for a, b, hi, lo in c["steps"][m]:
                        if lo:
                            if hi:
                                dve.wait_ge(sorted_ops[n], base + tops[a][1])
                            v_.tensor_tensor(c["buf"][:, buf[b], :], c["buf"][:, buf[a], :], c["buf"][:, buf[b], :],
                                             ALU.min).then_inc(sorted_ops[n], 1)
                            done[n] += 1
                    for a, b, hi, lo in c["steps"][m]:
                        if hi:
                            spare.append(buf[a])
                            buf[a] = tops[a][0]

                def weights():
                    v_.tensor_scalar(row(AM), deg_sorted[parity][:, 0, :], -1.0, None, ALU.add)
                    settle()
                    wtf = wt[:, :, :].rearrange("p t k -> p (t k)")
                    for n, (tau, weight) in enumerate(TAUS):
                        v_.tensor_scalar(row(A0), row(AM), -(1.0 - tau), None, ALU.mult)
                        settle()
                        v_.tensor_tensor(wt[:, :, :], count_row[:, 0:K1].unsqueeze(1).broadcast_to([P, U, K1]),
                                         over_tiles(row(A0), K1), ALU.add)
                        settle()
                        v_.scalar_tensor_tensor(wtf, wtf, -1.0, wtf, ALU.mult, ALU.max)
                        settle()
                        v_.tensor_scalar(wt[:, :, :], wt[:, :, :], -1.0, 1.0, ALU.mult, ALU.add)
                        settle()
                        dst = wt if n else wq
                        v_.tensor_scalar(dst[:, :, :], wt[:, :, :], 0.0, weight, ALU.max, ALU.mult)
                        settle()
                        if n:
                            v_.tensor_tensor(wq[:, :, :], wq[:, :, :], wt[:, :, :], ALU.add)
                            settle()

                def pick_slot(k):
                    lo = min(c["tiles"][0] for c in CLASSES if k < c["k"]) // W * R
                    if k >= PICKS1:
                        dve.wait_ge(fetched1_ps, g * K1 + (k - PICKS1 + 1))
                    v_.tensor_scalar(pick1[:, k % PICKS1, :, lo:N], by_tile(slot1[:, :, :, :])[:, :, lo:N],
                                     float(k + 1), None, ALU.is_equal).then_inc(pick1_ready, 1)

                pick_slot(0)
                weights()
                for k in range(K1 + SORT_LAG):
                    if k < K1:
                        yield "slot", k
                        if k + 1 < K1:
                            pick_slot(k + 1)
                    for i, (slot, steps) in enumerate(sorts):
                        if slot == k - SORT_LAG:
                            yield "sort", i
                            dve.wait_ge(fetched1_sb, g * K1 + (slot + 1))
                            for n, m in steps:
                                sort_step(n, m)
                for n, c in enumerate(CLASSES):
                    yield "quantile", n
                    t0, t1 = c["tiles"]
                    dve.wait_ge(sorted_ops[n], g * c["ops"] + c["ops"])
                    buf, term = bufs[n], spares[n][0:2]
                    acc, D = agg[:, t0:t1, :], used_places(c["k"])

                    def tiles(i):
                        return c["buf"][:, i, :].rearrange("p (t c) -> p t c", c=F)

                    for d in range(D + 1):
                        if d < D:
                            v_.tensor_tensor(tiles(term[d % 2]) if d else acc, tiles(buf[d]),
                                             wq[:, t0:t1, d].unsqueeze(2).broadcast_to([P, t1 - t0, F]), ALU.mult)
                        if d >= 2:
                            v_.tensor_tensor(acc, acc, tiles(term[(d - 1) % 2]), ALU.add)
                        settle()
                yield "agg"
                dve.nop(nofuse=True)
                long_group = dve.value_load(is_long[parity][0:1, 0:1])
                with dve.If(long_group > 0):
                    general_quantiles(g)
                with dve.Else():
                    dve.sem_inc(valid_used, T)
                    dve.sem_inc(row_used, T * F + 1)
                settle()
                split_in_three(agg[:, :, :], [aggp[:, i] for i in range(3)], xcA[:, :, :]).then_inc(agg_ready, 1)
                yield "x2"
                dve.wait_ge(y1_ps, g * G + G)
                v_.tensor_tensor(xcA[:, :, :], ps[:, 3, :].rearrange("p (t c) -> p t c", c=F), over_tiles(row(AMC)),
                                 ALU.mult)
                settle()
                v_.tensor_tensor(xs[parity][:, :, :], xs[parity][:, :, :], xcA[:, :, :], ALU.add).then_inc(x2_ready, 1)
                settle()

            def B_(g, parity, turn):
                x_ = xs[parity][:, :, :]
                hh = hB[:, :, :]

                def row(i):
                    return smB[:, i, :]

                def pick_unit(i):
                    k, q0, q1 = UNITS[i]
                    if i >= PICKS2:
                        dve.wait_ge(fetched2_ps, g * NU + (i - PICKS2 + 1))
                    v_.tensor_scalar(pick2[:, i % PICKS2, :, 0:(q1 - q0) * R],
                                     by_tile(slot2[parity][:, :, :, :])[:, :, q0 * R:q1 * R],
                                     float(k + 1), None, ALU.is_equal).then_inc(pick2_ready, 1)

                yield "layernorm2"
                layernorm_variance(x_, xcB, sqB, smB, (ST0, ST1, ST2, ST3), varB)
                yield "h2"
                layernorm_relu(hB, xcB, smB, (ST0, ST1, ST2, ST3), stdB, 0, g)
                settle()
                split_in_three(hh, [hpB[:, :, i, :] for i in range(3)], xcB[:, :, :]).then_inc(h2_ready, 1)
                v_.tensor_tensor(row(DK), deg_sorted[parity][:, 1, :], caps[:, 1, :], ALU.subtract)
                v_.tensor_tensor(sqB[:, :, :], over_tiles(deg_node[parity][:, :]),
                                 b2_all[:, :].unsqueeze(1).broadcast_to([P, T, F]), ALU.mult)
                settle()
                v_.tensor_tensor(x_, x_, sqB[:, :, :], ALU.add)
                for w in range(W):
                    tw = slice(w * T // W, (w + 1) * T // W)
                    yield ("uv", 4) if w == 0 else "uv_parts"
                    dve.wait_ge(v_sb, g * G + 2 * w + 2)
                    split_rest(v2[:, tw, :], [vp[:, tw, i, :] for i in range(3)], acc2[:, tw, :]
                                   ).then_inc(parts2_ready, 1)
                pick_unit(0)
                pick_unit(1)
                settle()
                dve.wait_ge(u_sb, g * W + W)
                split_rest(u2, up, acc2).then_inc(up_ready, 1)
                settle()
                v_.scalar_tensor_tensor(acc2, u2, 0.0, over_tiles(row(DK), H2), ALU.max, ALU.mult)
                settle()

                def take(j):
                    _, q0, q1 = UNITS[j]
                    nq = q1 - q0
                    dve.wait_ge(fetched2_ps, g * NU + (j + 1))
                    if j >= 2:
                        dve.wait_ge(summed2, g * NU + (j - 1))
                    bank = 4 + 2 * (j % 2)
                    v_.tensor_tensor(t2[:, j % 2, 0:nq * W].rearrange("p (a b) c -> p a (b c)", a=nq),
                                     u2[:, q0 * W:q1 * W, :].rearrange("p (a b) c -> p a (b c)", a=nq),
                                     ps[:, bank:bank + nq, 0:W * H2], ALU.add).then_inc(taken2, 1)

                def add(j):
                    _, q0, q1 = UNITS[j]
                    if j < DIRECT:
                        dve.wait_ge(taken2, g * DIRECT + (j + 1))
                    else:
                        dve.wait_ge(fetched2_ps, g * NU + (j + 1))
                    before = [i for i in range(j) if UNITS[i][1] < q1 and q0 < UNITS[i][2]]
                    if before:
                        dve.wait_ge(summed2, g * NU + (before[-1] + 1))
                    bank = 4 + 2 * (j % 2)
                    a2 = acc2[:, q0 * W:q1 * W, :].rearrange("p (a b) c -> p a (b c)", b=W)
                    h = t2[:, j % 2, 0:(q1 - q0) * W].rearrange("p (a b) c -> p a (b c)", b=W) if j < DIRECT else \
                        ps[:, bank:bank + q1 - q0, 0:W * H2]
                    v_.scalar_tensor_tensor(a2, h, 0.0, a2,
                                            ALU.max, ALU.add).then_inc(summed2, 1)

                for i in range(NU):
                    yield "unit", i
                    if i + 2 < NU:
                        pick_unit(i + 2)
                    if 1 <= i <= DIRECT:
                        take(i - 1)
                    if 2 <= i < DIRECT + 2:
                        add(i - 2)
                    if i > DIRECT:
                        add(i - 1)
                yield "sum2"
                add(NU - 1)
                dve.nop(nofuse=True)
                long_group = dve.value_load(is_long[parity][0:1, 0:1])
                with dve.If(long_group > 0):
                    general_relu_sum(g, parity)
                with dve.Else():
                    dve.sem_inc(more_picked, MORE)
                    dve.sem_inc(more_summed, MORE)
                settle()
                v_.tensor_copy(overB[:, :], overB[:, :]).then_inc(acc2_ready, 1)
                yield "y2"
                dve.wait_ge(ysort_sb, g + 1)
                split_rest(y_sorted.rearrange("p u c -> p (u c)"), [yp[:, i, :] for i in range(3)],
                           sqB[:, :, :].rearrange("p t c -> p (t c)")).then_inc(yp_ready, 1)
                yield "layernorm3"
                dve.wait_ge(y2_ps, g + 1)
                for s in range(2):
                    xv = x_.rearrange("p (w s a) c -> p w s (a c)", s=2, a=HALVES)[:, :, s, :]
                    v_.tensor_tensor(xv, xv, ps[:, 5 + s, 0:W * HALVES * F].rearrange("p (w n) -> p w n", w=W), ALU.add)
                settle()
                layernorm_variance(x_, xcB, sqB, smB, (ST0, ST1, ST2, ST3), varB)
                yield "h3"
                layernorm_relu(hB, xcB, smB, (ST0, ST1, ST2, ST3), stdB, 1, g)
                settle()

                def dot_with(dst, a, b):
                    v_.tensor_tensor(sqB[:, :, :], a, b, ALU.mult)
                    settle()
                    v_.reduce_sum(dst, sqB[:, :, :], AX.X)
                    settle()

                def ts(dst, src, s1, s2, op0, op1=ALU.bypass):
                    i = v_.tensor_scalar(row(dst), row(src), s1, s2, op0, op1) if s2 is not None else \
                        v_.tensor_scalar(row(dst), row(src), s1, None, op0)
                    settle()
                    return i

                def tt(dst, a, b, op):
                    i = v_.tensor_tensor(row(dst), row(a), row(b), op)
                    settle()
                    return i

                dot_with(row(X2), hh, hh)
                v_.tensor_copy(row(M1), row(X2)).then_inc(small_ready, 1)
                dot_with(row(WS), hh, att_w[:, 0, :].unsqueeze(1).broadcast_to([P, T, F]))
                dot_with(row(WL), hh, att_w[:, 1, :].unsqueeze(1).broadcast_to([P, T, F]))
                ts(BM, X2, -1.0, 1.0, ALU.mult, ALU.add)
                ts(LAM, BM, MIN_NORM, None, ALU.max)
                tt(LB, LAM, BM, ALU.mult)
                tt(LW, LAM, WL, ALU.mult)
                ts(NLW, LW, -1.0, None, ALU.mult)
                ts(S0, X2, -2.0, 1.0, ALU.mult, ALU.add)
                tt(S1, S0, X2, ALU.add)
                tt(DF, BM, S1, ALU.subtract)
                tt(S1, X2, X2, ALU.mult)
                tt(DD, S0, S1, ALU.add)
                ts(DD, DD, MIN_NORM, None, ALU.max)
                v_.reciprocal(row(S3), row(DD))
                settle()
                tt(DF, DF, S3, ALU.mult)
                v_.scalar_tensor_tensor(row(S4), row(DF), -1.0, row(DF), ALU.mult, ALU.max)
                settle()
                yield "values"
                dve.wait_ge(small_done, g * SMALL + 1)
                tt(SN, S4, NORM, ALU.mult)
                ts(SN, SN, MIN_NORM, None, ALU.max)
                v_.tensor_scalar(row(S2), row(SN), CLIP, None, ALU.min).then_inc(small_ready, 1)
                v_.reciprocal(row(S4), row(SN))
                settle()
                tt(S4, S4, DF, ALU.mult)
                tt(S4, S4, LAM, ALU.mult)
                tt(S4, S4, WS, ALU.mult)
                yield "tokens"
                dve.wait_ge(small_done, g * SMALL + 2)
                tt(S0, S0, S1, ALU.subtract)
                tt(S0, S0, S4, ALU.mult)
                v_.tensor_scalar(row(CC), row(S0), 0.5, att_c[:, 0:1], ALU.mult, ALU.add)
                v_.tensor_copy(tok[:, 0, :, 0:F], hh)
                v_.tensor_scalar(tok[:, 1, :, 0:F], hh, -2.0, None, ALU.mult)
                v_.tensor_scalar(tok[:, 2, :, 0:F], hh, -2.0, None, ALU.mult)
                v_.scalar_tensor_tensor(tok[:, 3, :, 0:F], hh, 2.0, over_tiles(row(LW)), ALU.mult, ALU.mult)
                for which, rows in enumerate(((X2, None, WL), (X2, None, 0.0), (None, X2, 0.0), (NLW, NLW, LB))):
                    for c, r in enumerate(rows):
                        dst = tok[:, which, :, F + c]
                        if r is None or r == 0.0 and isinstance(r, float):
                            v_.memset(dst, 1.0 if r is None else 0.0)
                        else:
                            v_.tensor_copy(dst, row(r))
                settle()
                v_.tensor_copy(row(M1), row(CC)).then_inc(tok_ready, 1)

                for i in range(G + 2):
                    yield "pair", i, 0
                    if 1 <= i <= G:
                        j = i - 1
                        dve.wait_ge(pair_ps, g * G + (j + 1))
                        v_.tensor_scalar(bd[:, j], bank_pairs(4), MIN_NORM, None, ALU.max)
                        v_.tensor_scalar(bn[:, j], bank_pairs(5), MIN_SQ, None, ALU.max).then_inc(clamped, 1)
                    if i >= 2:
                        j = i - 2
                        dve.wait_ge(exps_sb, g * G + (j + 1))
                        v_.tensor_scalar(bq[:, j], bq[:, j], CLIP, None, ALU.min).then_inc(s_clipped, 1)
                for i in range(G + 2):
                    yield "logit", i
                    if i == 0:
                        dve.wait_ge(cb_sb, g + 1)
                        dve.wait_ge(hz_sb, g * G + G)
                    if i < G:
                        dve.wait_ge(diff_ready, g * G + (i + 1))
                        v_.scalar_tensor_tensor(f2(bd[:, i]), f2(bd[:, i]), 0.5, f2(bn[:, i]), ALU.mult, ALU.mult)
                    if 1 <= i <= G:
                        v_.tensor_tensor(bz[:, i - 1], bz[:, i - 1], bd[:, i - 1], ALU.mult)
                    if i >= 2:
                        v_.tensor_tensor(bz[:, i - 2], bz[:, i - 2],
                                         cb[:, i - 2].unsqueeze(1).broadcast_to([P, HALVES, N]), ALU.add
                                         ).then_inc(z_ready, 1)
                    settle()
                v_.tensor_copy(feat3[:, :, 0:F], hh)
                v_.tensor_scalar(feat3[:, :, F], row(X2), 1.0, None, ALU.add).then_inc(feat3_ready, 1)
                yield "weights"
                for i in range(G):
                    dve.wait_ge(att_ready, g * G + (i + 1))
                    v_.tensor_tensor(bd[:, i], bd[:, i], bz[:, i], ALU.mult).then_inc(weight_ready, 1)

                yield "support"
                dve.wait_ge(support_sb, g + 1)
                s1 = sp[:, :, 0:F]
                dot_with(row(S0), hh, s1)
                v_.scalar_tensor_tensor(row(S1), row(S0), -2.0, sp[:, :, F], ALU.mult, ALU.add)
                settle()
                tt(S1, S1, LAM, ALU.mult)
                v_.tensor_tensor(y3, s1, over_tiles(row(LB)), ALU.mult)
                v_.tensor_tensor(z3, hh, over_tiles(row(S1)), ALU.mult)
                settle()
                v_.tensor_tensor(y3, y3, z3, ALU.subtract)
                settle()
                v_.tensor_scalar(y3, y3, CLAMP, -CLAMP, ALU.min, ALU.max)
                settle()
                dot_with(row(S0), y3, y3)
                v_.tensor_scalar(row(S0), row(S0), MIN_NORM * MIN_NORM, None, ALU.max).then_inc(small_ready, 1)
                v_.reciprocal(row(S4), row(LAM))
                settle()
                yield "step"
                dve.wait_ge(small_done, g * SMALL + 3)
                v_.tensor_tensor(row(S2), row(S1), row(S4), ALU.mult).then_inc(small_ready, 1)
                v_.reciprocal(row(S5), row(S1))
                settle()
                yield "tanh"
                dve.wait_ge(small_done, g * SMALL + 4)
                tt(S5, S5, S3, ALU.mult)
                v_.tensor_tensor(y3, y3, over_tiles(row(S5)), ALU.mult)
                settle()
                dot_with(row(S2), y3, y3)
                dot_with(row(S3), hh, y3)
                ts(S4, S3, 2.0, 1.0, ALU.mult, ALU.add)
                tt(S5, S4, S2, ALU.add)
                tt(S2, S2, X2, ALU.mult)
                tt(S4, S4, S2, ALU.add)
                ts(S4, S4, MIN_NORM, None, ALU.max)
                v_.reciprocal(row(S3), row(S4))
                settle()
                tt(S5, S5, S3, ALU.mult)
                tt(S4, BM, S3, ALU.mult)
                v_.tensor_tensor(z3, hh, over_tiles(row(S5)), ALU.mult)
                v_.tensor_tensor(y3, y3, over_tiles(row(S4)), ALU.mult)
                settle()
                v_.tensor_tensor(y3, y3, z3, ALU.add)
                settle()
                dot_with(row(S0), y3, y3)
                v_.tensor_scalar(row(S0), row(S0), MIN_NORM * MIN_NORM, None, ALU.max).then_inc(small_ready, 1)
                yield "moved"
                dve.wait_ge(small_done, g * SMALL + 5)
                v_.reciprocal(row(S2), row(S1))
                settle()
                ts(S2, S2, MAXNORM, 1.0, ALU.mult, ALU.min)
                v_.tensor_tensor(y3, y3, over_tiles(row(S2)), ALU.mult)
                settle()
                v_.tensor_tensor(x_, x_, y3, ALU.add).then_inc(out_ready, 1)
                settle()

            run(dve, A, B_)

        @block.tensor
        def _(pe):
            t_ = nc.tensor

            def mm(o, lhsT, rhs, start=True, stop=True):
                return t_.matmul(o, lhsT, rhs, start=start, stop=stop)

            def held():
                pe.nop(nofuse=True)

            def half(a):
                return slice(a * P, (a + 1) * P)

            def side(s):
                return slice(s * R, (s + 1) * R)

            def quarter(q):
                return slice(q * R, (q + 1) * R)

            def running_count(mask):
                for b in range(G):
                    mm(ps[:, b, 0:N], tri[:, :], mask[:, b, 0, :])
                    mm(ps[:, b, N:2 * N], onesb[:, :], mask[:, b, 0, :], stop=False)
                    last = mm(ps[:, b, N:2 * N], tri[:, :], mask[:, b, 1, :], start=False)
                return last

            def sum_of(o, terms):
                for n, (l, r) in enumerate(terms):
                    last = mm(o, l, r, start=n == 0, stop=n == len(terms) - 1)
                return last

            def general_rows(g):
                pe.wait_ge(fetched1_sb, g * K1 + K1)
                held()
                for t in range(T):
                    b, a = divmod(t, 2)
                    if t >= 1:
                        pe.wait_ge(valid_used, g * T + t)
                        held()
                    for c in range(HALVES):
                        last = t_.transpose(psb[:, 1, half(c)], slot1[:, b, c, half(a)], identb[:, :])
                    last.then_inc(valid_ps, 1)
                    with pe.Fori(0, F) as c:
                        pe.wait_ge(row_used, g * (T * F + 1) + c + (t * F + 1))
                        for j in range(HALVES):
                            for part in range(3):
                                last = mm(ps[:, 2, half(j)],
                                          hpA[:, 2 * b + j, part, bass.ds(c, 1)].broadcast_to([P, P]), identb[:, :],
                                          start=part == 0, stop=part == 2)
                        last.then_inc(row_ps, 1)

            def fetch2(pick, bank_of, cols_of, tiles, start=True):
                for q, w, at in tiles:
                    for c in range(HALVES):
                        for part in range(3):
                            for s in range(2):
                                last = mm(ps[side(s), bank_of(q), cols_of(w)], pick(2 * w + s, c)[:, at:at + R],
                                          vp[:, 2 * (2 * w + s) + c, part, :],
                                          start=start and c == 0 and part == 0,
                                          stop=c == 1 and part == 2 and (start or w == W - 1))
                return last

            def general_fetch(g):
                at = 0
                for q, k2 in enumerate(K2Q):
                    for w in range(W):
                        with pe.Fori(0, N - k2) as k:
                            pe.wait_ge(more_picked, g * MORE + k + (at + 1))
                            held()
                            fetch2(lambda b, c: pick2[:, 0, 2 * (b % 2) + c, :], lambda q: 4, lambda w: slice(0, H2),
                                   [(q, w, 0)]).then_inc(more_ps, 1)
                        at += N - k2

            pe.wait_ge(const_loaded, 16 * NCONST)
            pe.wait_ge(const_made, MADE)
            pe.wait_ge(mask_cast, 2)
            t_.transpose(ps[:, 0, 0:B * HALVES], mask_f[:, :], identf[0:B * HALVES, 0:B * HALVES]).then_inc(mask_T, 1)
            pe.wait_ge(mask_taken, 1)
            one_row = onesf[0:1, :]

            def A(g, parity, turn):
                yield "masks"
                pe.wait_ge(adj_loaded, g * 16 + 16)
                if not is_first(g):
                    pe.wait_ge(x2_ready, g)
                held()
                for b in range(G):
                    for a in range(HALVES):
                        for c in range(HALVES):
                            last = t_.transpose(ps[:, b, c * N + a * P:c * N + (a + 1) * P],
                                                adj_in[:, 2 * b + a, half(c)], identf[:, :])
                    last.then_inc(adjT_ps, 1)
                yield "masksT"
                pe.wait_ge(nb_ready, g + 1)
                held()
                for n, mask in enumerate((nb_T, any_T)):
                    for t in range(T):
                        b, a = divmod(t, 2)
                        sum_of(ps[:, 0, n * T + t:n * T + t + 1], [(mask[:, b, c, half(a)], onesb[:, 0:1])
                                                                   for c in range(HALVES)])
                for b in range(G):
                    last = sum_of(ps[:, 1 + b // 2, (b % 2) * N:(b % 2 + 1) * N],
                                  [(onesb[:, :], any_T[:, b, c, :]) for c in range(HALVES)])
                last.then_inc(counts_ps, 1)
                yield "keys"
                pe.wait_ge(counts_taken, g + 1)
                held()
                for t in range(T):
                    b, a = divmod(t, 2)
                    mm(ps[:, b, a * N:a * N + P], nb_T[:, b, 0, half(a)], tri[:, :])
                    last = sum_of(ps[:, b, a * N + P:(a + 1) * N], [(nb_T[:, b, 0, half(a)], onesb[:, :]),
                                                                    (nb_T[:, b, 1, half(a)], tri[:, :])])
                last.then_inc(cum_ps, 1)
                yield "gone"
                pe.wait_ge(gone_ready, g + 1)
                held()
                for t in range(T):
                    b, a = divmod(t, 2)
                    sum_of(ps[:, 0, t:t + 1], [(less[:, b, c, half(a)], onesb[:, 0:1]) for c in range(HALVES)])
                for w in range(W):
                    for s in range(2):
                        last = sum_of(ps[side(s), 1, w * N:(w + 1) * N],
                                      [(onesb[:, 0:R], less[:, 2 * w + s, c, :]) for c in range(HALVES)])
                last.then_inc(rank_ps, 1)
                for b in range(G):
                    for a in range(HALVES):
                        for c in range(HALVES):
                            o = (b % 2) * 2 * N + c * N + a * P
                            last = t_.transpose(psb[:, 2 + b // 2, o:o + P], gone[:, b, a, half(c)], identb[:, :])
                last.then_inc(goneT_ps, 1)
                yield "ranks"
                pe.wait_ge(val_ready, g + 1)
                for m, mask in enumerate((val_m, any_m)):
                    for b in range(G):
                        if m == 1:
                            pe.wait_ge(sortmask_sb, g * (2 * G) + (b + 1))
                        held()
                        for c in range(HALVES):
                            last = sum_of(ps[:, b, c * N:(c + 1) * N],
                                          [(mask[:, b, a, half(c)], perm[:, b, a, :]) for a in range(HALVES)])
                        last.then_inc(sortmask_ps, 1)
                yield "count"
                pe.wait_ge(sortmask_sb, g * (2 * G) + 2 * G)
                held()
                running_count(val_s).then_inc(cum1_ps, 1)
                yield "slot1"
                pe.wait_ge(slot1_ready, g + 1)
                held()
                running_count(any_s).then_inc(cum2_ps, 1)
                yield "slot2"
                pe.wait_ge(slot2_ready, g + 1)
                held()
                for n, mask in enumerate((val_s, any_s)):
                    for q in range(Q):
                        for w in range(W):
                            at = n * U + q * W + w
                            for s in range(2):
                                last = sum_of(ps[side(s), 0, at:at + 1], [(mask[:, 2 * w + s, c, quarter(q)],
                                                                           onesb[:, 0:1]) for c in range(HALVES)])
                last.then_inc(deg_ps, 1)
                yield "lengths"
                pe.wait_ge(over_ready, g + 1)
                held()
                t_.transpose(ps[0:1, 1, 0:P], over[:, 0:1], identf[:, :]).then_inc(over_ps, 1)

                for i in range(G + 2):
                    yield "layer0", i
                    if i == 0:
                        pe.wait_ge(long_ready, g + 1)
                        pe.wait_ge(h0_ready, g + 1)
                    if i < G:
                        held()
                        sum_of(ps[0:F, i % 2, N:2 * N], [(hA[:, 2 * i + c, :], adjT[parity][:, i, c, :])
                                                         for c in range(HALVES)])
                        for a in range(HALVES):
                            last = t_.transpose(ps[0:F, i % 2, half(a)], hA[:, 2 * i + a, :], identf[:, :])
                        last.then_inc(feat0_ps, 1)
                    if i >= 2:
                        layer0_out(g, i - 2)
                    if 1 <= i <= G:
                        r = (i - 1) % 2
                        pe.wait_ge(feat0_sb, g * G + i)
                        held()
                        sum_of(ps[0:F, 2, r * N:(r + 1) * N], [(w1_0[:, e, :], feat[:, r, e, :]) for e in range(2)]
                               ).then_inc(pre0_ps, 1)
                for k in range(K1):
                    yield "slot", k
                    if k == 0:
                        pe.wait_ge(parts1_ready, g + 1)
                    pe.wait_ge(pick1_ready, g * K1 + (k + 1))
                    if k >= 4:
                        pe.wait_ge(fetched1_sb, g * K1 + (k - 3))
                    held()
                    lo = min(c["tiles"][0] for c in CLASSES if k < c["k"])
                    for u in range(lo, U):
                        q, w = divmod(u, W)
                        for c in range(HALVES):
                            for part in range(3):
                                for s in range(2):
                                    b = 2 * w + s
                                    last = mm(ps[side(s), k % 4, u * F:(u + 1) * F],
                                              pick1[:, k % PICKS1, 2 * b + c, quarter(q)], hpA[:, 2 * b + c, part, :],
                                              start=c == 0 and part == 0, stop=c == 1 and part == 2)
                    last.then_inc(fetched1_ps, 1)
                yield "agg"
                pe.wait_ge(long_ready, g + 1)
                held()
                long_group = pe.value_load(is_long[parity][0:1, 0:1])
                with pe.If(long_group > 0):
                    general_rows(g)
                with pe.Else():
                    pe.sem_inc(valid_ps, T)
                    pe.sem_inc(row_ps, T * F)
                for i in range(G + 2):
                    yield "mlp", i
                    if i == 0:
                        pe.wait_ge(agg_ready, g + 1)
                    if i < G:
                        held()
                        w, s = divmod(i, 2)
                        o = ps[0:F, i % 2, :]
                        for part in range(3):
                            for q in range(Q):
                                mm(o[:, 0:N], aggp[side(s), part, q * W + w, :], permT[side(s), q, w, :],
                                   start=part == 0 and q == 0, stop=False)
                            for a in range(HALVES):
                                last = mm(o[:, half(a)], hpA[:, 2 * i + a, part, :], identb[:, :], start=False,
                                          stop=part == 2 and a == 1)
                        last.then_inc(aggT_ps, 1)
                    if i >= 2:
                        layer1_out(g, i - 2)
                    if 1 <= i <= G:
                        r = (i - 1) % 2
                        pe.wait_ge(aggT_sb, g * G + i)
                        held()
                        mm(ps[:, 2, r * N:(r + 1) * N], w1_1[:, :], feat[:, r, 0, :]).then_inc(hid_ps, 1)

            def layer0_out(g, b):
                pe.wait_ge(tanh_sb, g * G + (b + 1))
                held()
                for a in range(HALVES):
                    t = 2 * b + a
                    last = sum_of(ps[:, 3, t * F:(t + 1) * F], [(tanh_t[:, b % 2, half(a)], w2_0[:, :]),
                                                                (one_row, brow[:, 0, :])])
                last.then_inc(dh0_ps, 1)

            def layer1_out(g, b):
                pe.wait_ge(hid_sb, g * G + (b + 1))
                held()
                for a in range(HALVES):
                    t = 2 * b + a
                    last = sum_of(ps[:, 3, t * F:(t + 1) * F], [(hid[:, b % 2, half(a)], w2_1[:, :]),
                                                                (one_row, brow[:, 1, :])])
                last.then_inc(y1_ps, 1)

            def B_(g, parity, turn):
                for i in range(7):
                    yield "uv", i
                    if i == 0:
                        pe.wait_ge(h2_ready, g + 1)
                        held()
                    if i in (1, 2, 4, 5):
                        b = (None, 0, 1, None, 2, 3)[i]
                        r = b % 2
                        pe.wait_ge(h2T_sb, g * G + (b + 1))
                        if b >= 2:
                            pe.wait_ge(v_sb, g * G + (b - 1))
                        held()
                        for a in range(HALVES):
                            last = mm(ps[:, 6 + r, a * H2:(a + 1) * H2], featB[:, r, 0, half(a)], w1_2[:, 1, :])
                        last.then_inc(v_ps, 1)
                    if i in (2, 6):
                        w = i // 4
                        if w == 1:
                            pe.wait_ge(v_sb, g * G + G)
                            held()
                        for q in range(Q):
                            for s_ in range(2):
                                o = ps[side(s_), 4 + 2 * w + q // 2, (q % 2) * H2:(q % 2 + 1) * H2]
                                last = sum_of(o, [(featB[:, s_, 1, quarter(q)], wsum_2[:, :]),
                                                  (one_row[:, 0:R], brow2[:, :])])
                        last.then_inc(u_ps, 1)
                    if i in (0, 1, 3, 4):
                        b = (0, 1, None, 2, 3)[i]
                        r = b % 2
                        if b == 2:
                            pe.wait_ge(u_sb, g * W + 1)
                            held()
                        for a in range(HALVES):
                            t_.transpose(ps[0:F, 4, r * N + a * P:r * N + (a + 1) * P], hB[:, 2 * b + a, :],
                                         identf[:, :])
                        sum_of(ps[0:F, 5, r * N:(r + 1) * N], [(hpB[:, 2 * b + a, part, :], perm[:, b, a, :])
                                                               for a in range(HALVES) for part in range(3)]
                               ).then_inc(h2T_ps, 1)
                for i, (k, q0, q1) in enumerate(UNITS):
                    yield "unit", i
                    if i == 0:
                        pe.wait_ge(parts2_ready, g * W + W)
                        pe.wait_ge(up_ready, g + 1)
                    pe.wait_ge(pick2_ready, g * NU + (i + 1))
                    if 2 <= i < DIRECT + 2:
                        pe.wait_ge(taken2, g * DIRECT + (i - 1))
                    elif i >= 2:
                        pe.wait_ge(summed2, g * NU + (i - 1))
                    held()
                    for q in range(q0, q1) if i >= DIRECT else ():
                        for part in range(3):
                            mm(ps[:, 4 + 2 * (i % 2) + q - q0, 0:W * H2], identb[:, :],
                               up[part][:, q * W:(q + 1) * W, :].rearrange("p w c -> p (w c)"), start=part == 0,
                               stop=False)
                    fetch2(lambda b, c: pick2[:, i % PICKS2, 2 * b + c, :], lambda q: 4 + 2 * (i % 2) + q - q0,
                           lambda w: slice(w * H2, (w + 1) * H2),
                           [(q, w, (q - q0) * R) for q in range(q0, q1) for w in range(W)],
                           start=i < DIRECT).then_inc(fetched2_ps, 1)
                yield "sum2"
                pe.wait_ge(summed2, g * NU + NU)
                held()
                long_group = pe.value_load(is_long[parity][0:1, 0:1])
                with pe.If(long_group > 0):
                    general_fetch(g)
                with pe.Else():
                    pe.sem_inc(more_ps, MORE)
                pe.wait_ge(acc2_ready, g + 1)
                held()
                for w in range(W):
                    for c in range(2):
                        for q in range(Q):
                            last = t_.transpose(ps[0:H2 // 2, 4 + 2 * w + c, q * P:(q + 1) * P],
                                                acc2[:, q * W + w, c * (H2 // 2):(c + 1) * (H2 // 2)], identf[:, :])
                    last.then_inc(acc2T_ps, 1)
                yield "y_sorted"
                pe.wait_ge(acc2T_sb, g * W + W)
                held()
                for q in range(Q):
                    for w in range(W):
                        u = q * W + w
                        last = sum_of(ps[:, 4, u * F:(u + 1) * F],
                                      [(acc2T[:, w, c * 512 + q * P:c * 512 + (q + 1) * P], w2_2[:, c, :])
                                       for c in range(2)])
                last.then_inc(ysort_ps, 1)
                yield "y2"
                pe.wait_ge(yp_ready, g + 1)
                pe.wait_ge(permT_saved, g + 1)
                held()
                for t in range(T):
                    b, a = divmod(t, 2)
                    w, s = divmod(b, 2)
                    at = (2 * w + a) * F
                    last = sum_of(ps[:, 5 + s, at:at + F],
                                  [(permT2[side(s), q, w, half(a)],
                                    yp[side(s), part, (q * W + w) * F:(q * W + w + 1) * F])
                                   for q in range(Q) for part in range(3)])
                last.then_inc(y2_ps, 1)

                yield "tokens"
                pe.wait_ge(tok_ready, g + 1)
                held()
                t_.transpose(ps[0:T, 4, 0:P], smB[:, M1, :], identf[:, :]).then_inc(cT_ps, 1)
                yield "columns"
                pe.wait_ge(cT_sb, g + 1)
                held()
                for t in range(T):
                    b, a = divmod(t, 2)
                    last = mm(ps[:, 5 + b // 2, (b % 2) * N + a * P:(b % 2) * N + (a + 1) * P],
                              identf[0:T, t:t + 1].broadcast_to([T, P]), cT[:, :])
                last.then_inc(cb_ps, 1)
                for i in range(G):
                    for e in range(2):
                        yield "pair", i, e
                        if i or e:
                            pe.wait_ge(LR_sb, g * (2 * G) + (2 * i + e))
                        held()
                        for which in range(2):
                            for a in range(HALVES):
                                o = which * N + a * P
                                last = t_.transpose(ps[0:FX, 7, o:o + P], tok[:, 2 * e + which, 2 * i + a, :],
                                                    identf[:, :])
                        last.then_inc(LR_ps, 1)
                    yield "pair", i, 2
                    pe.wait_ge(LR_sb, g * (2 * G) + (2 * i + 2))
                    if i == 0:
                        pe.wait_ge(cb_sb, g + 1)
                    else:
                        pe.wait_ge(clamped, g * G + i)
                        pe.wait_ge(hz_sb, g * G + i)
                    held()
                    for m in range(3):
                        for a in range(HALVES):
                            last = mm(ps[:, 4 + m, a * N:(a + 1) * N], LR[:, 0, half(a)], LR[:, 1 + m, :])
                    last.then_inc(pair_ps, 1)
                yield "weights"
                pe.wait_ge(feat3_ready, g + 1)
                for b in range(G):
                    pe.wait_ge(weight_ready, g * G + (b + 1))
                    held()
                    for a in range(HALVES):
                        t = 2 * b + a
                        last = sum_of(ps[:, 4 + t // 4, (t % 4) * P:(t % 4) * P + F + 1],
                                      [(bd[:, b, c, half(a)], feat3[:, 2 * b + c, :]) for c in range(HALVES)])
                last.then_inc(support_ps, 1)

            run(pe, A, B_)


def kernel(**inputs):
    import concourse.bacc as bacc
    from concourse.bass_utils import run_bass_kernel_spmd

    nc = bacc.Bacc("TRN2", target_bir_lowering=False, num_devices=1)
    arrays, args = {}, []
    for name in ("x", "adj", "nodemask", "L0_gnn_W1", "L0_gnn_b1", "L0_gnn_W2", "L0_gnn_b2",
                 "L1_gnn_W1", "L1_gnn_b1", "L1_gnn_W2", "L1_gnn_b2", "L2_gnn_W1", "L2_gnn_b1", "L2_gnn_W2",
                 "L2_gnn_b2", "L3_gnn_att_W", "L3_gnn_att_b"):
        a = np.ascontiguousarray(inputs[name])
        if a.dtype == np.bool_:
            a = a.view(np.uint8)
        arrays[f"in_{name}"] = a
        args.append(nc.dram_tensor(f"in_{name}", a.shape, mybir.dt.from_np(a.dtype), kind="ExternalInput").ap())
    args.append(nc.dram_tensor("out", (B, N, F), F32, kind="ExternalOutput").ap())
    program(nc, *args)
    result = run_bass_kernel_spmd(nc, [arrays], core_ids=[0])
    return result.results[0]["out"]
```
